# Optimizing a Trainium2 kernel written in Bass

```python
import numpy as np
import jax
import jax.numpy as jnp

def _softmax(x, axis=-1):
    return jax.nn.softmax(x, axis=axis)

def _gelu(x):
    return jax.nn.gelu(x, approximate=True)

def _silu(x):
    return jax.nn.silu(x)

def _sigmoid(x):
    return jax.nn.sigmoid(x)

def _layernorm(x, axis=-1, eps=1e-05):
    m = jnp.mean(x, axis=axis, keepdims=True)
    v = jnp.var(x, axis=axis, keepdims=True)
    return (x - m) / jnp.sqrt(v + eps)

def _scatter_add(tgt, idx, src, axis=0):
    return tgt.at[idx].add(src)

def _segment_sum(src, seg, n):
    return jax.ops.segment_sum(src, seg, n)
kernel_name = 'mk_macaron_d2_jaxref_r8_3f34ee'

def setup_inputs(seed: int=0):
    np.random.seed(seed)
    _w = jnp.asarray

    def _L0_attn_setup():
        import jax, jax.numpy as jnp
        import numpy as np
        D_MODEL = 128
        N_HEADS = 16
        N_KV_HEADS = 4
        HEAD_DIM = 64
        S = 4
        W = 32
        B = 2
        T = 256

        def _sink_mask(seq_len, sink, window):
            t = jnp.arange(seq_len)
            i = t[:, None]
            j = t[None, :]
            sink_band = j < min(sink, seq_len)
            window_band = j >= jnp.maximum(i - window + 1, 0)
            causal = j <= i
            return causal & (sink_band | window_band)
        key = jax.random.key(seed)
        ks = jax.random.split(key, 5)
        scale = 0.02
        X = jax.random.normal(ks[0], (B, T, D_MODEL), dtype=jnp.float32)
        Wq = jax.random.normal(ks[1], (D_MODEL, N_HEADS * HEAD_DIM), dtype=jnp.float32) * scale
        Wk = jax.random.normal(ks[2], (D_MODEL, N_KV_HEADS * HEAD_DIM), dtype=jnp.float32) * scale
        Wv = jax.random.normal(ks[3], (D_MODEL, N_KV_HEADS * HEAD_DIM), dtype=jnp.float32) * scale
        Wo = jax.random.normal(ks[4], (N_HEADS * HEAD_DIM, D_MODEL), dtype=jnp.float32) * scale
        return {'X': X, 'Wq': Wq, 'Wk': Wk, 'Wv': Wv, 'Wo': Wo}
    _L0_attn_in = _L0_attn_setup()

    def _L0_ffn_setup():
        import jax, jax.numpy as jnp
        import numpy as np
        NUM_EXPERTS = 8
        TOP_K = 2
        D_MODEL = 128
        D_HID = 512
        BATCH, SEQ = (2, 256)
        key = jax.random.key(seed)
        ks = jax.random.split(key, 5)
        s = 0.02
        return {'x': jax.random.normal(ks[0], (BATCH, SEQ, D_MODEL), dtype=jnp.float32), 'Wg': jax.random.normal(ks[1], (D_MODEL, NUM_EXPERTS), dtype=jnp.float32) * s, 'bg': jnp.zeros((NUM_EXPERTS,), dtype=jnp.float32), 'W0': jax.random.normal(ks[2], (NUM_EXPERTS, D_MODEL, D_HID), dtype=jnp.float32) * s, 'b0': jnp.zeros((NUM_EXPERTS, D_HID), dtype=jnp.float32), 'W1': jax.random.normal(ks[3], (NUM_EXPERTS, D_MODEL, D_HID), dtype=jnp.float32) * s, 'b1': jnp.zeros((NUM_EXPERTS, D_HID), dtype=jnp.float32), 'W2': jax.random.normal(ks[4], (NUM_EXPERTS, D_HID, D_MODEL), dtype=jnp.float32) * s, 'b2': jnp.zeros((NUM_EXPERTS, D_MODEL), dtype=jnp.float32)}
    _L0_ffn_in = _L0_ffn_setup()

    def _L1_attn_setup():
        import jax, jax.numpy as jnp
        import numpy as np
        B, T, C = (8, 512, 128)
        LN_EPS = 1e-05
        NEG_INF = -1e+38

        def _ln(x, g, b):
            mu = jnp.mean(x, axis=-1, keepdims=True)
            var = jnp.mean(jnp.square(x - mu), axis=-1, keepdims=True)
            return (x - mu) * jax.lax.rsqrt(var + LN_EPS) * g + b

        def _shift(x):
            return jnp.concatenate([jnp.zeros_like(x[:, :1]), x[:, :-1]], axis=1)

        def _wkv(w, u, k, v):
            kt = jnp.moveaxis(k, 1, 0)
            vt = jnp.moveaxis(v, 1, 0)
            aa = jnp.zeros(k.shape[::2], k.dtype)
            bb = jnp.zeros(k.shape[::2], k.dtype)
            pp = jnp.full(k.shape[::2], NEG_INF, k.dtype)

            def step(carry, kv):
                aa, bb, pp = carry
                kk, vv = kv
                p = jnp.maximum(pp, u + kk)
                e1 = jnp.exp(pp - p)
                e2 = jnp.exp(u + kk - p)
                y = (e1 * aa + e2 * vv) / (e1 + e2)
                p2 = jnp.maximum(pp + w, w + kk)
                e1u = jnp.exp(pp + w - p2)
                e2u = jnp.exp(w + kk - p2)
                aa = e1u * aa + e2u * vv
                bb = e1u + e2u
                pp = p2 + jnp.log(bb)
                return ((aa, bb, pp), y)
            _, ys = jax.lax.scan(step, (aa, bb, pp), (kt, vt))
            return jnp.moveaxis(ys, 0, 1)
        key = jax.random.key(seed)
        ks = jax.random.split(key, 20)
        n = lambda i, sh, s=1.0: jax.random.normal(ks[i], sh, jnp.float32) * s
        un = lambda i, sh: jax.random.uniform(ks[i], sh, jnp.float32)
        return {'x': n(0, (B, T, C)), 'w': n(1, (C,), 0.01), 'u': n(2, (C,), 0.01), 'rk': un(3, (C,)), 'rv': un(4, (C,)), 'rr': un(5, (C,)), 'crk': un(6, (C,)), 'crr': un(7, (C,)), 'Wk': n(8, (C, C), 0.02), 'Wv': n(9, (C, C), 0.02), 'Wr': n(10, (C, C), 0.02), 'Wck': n(11, (4 * C, C), 0.02), 'Wcv': n(12, (C, 4 * C), 0.02), 'Wcr': n(13, (C, C), 0.02), 'ln1_g': jnp.ones((C,)), 'ln1_b': jnp.zeros((C,)), 'ln2_g': jnp.ones((C,)), 'ln2_b': jnp.zeros((C,))}
    _L1_attn_in = _L1_attn_setup()

    def _L1_ffn_setup():
        import jax, jax.numpy as jnp
        import numpy as np
        B, S, D, E, H, DO = (4, 256, 128, 8, 512, 128)
        TOP_K = 2
        LN_EPS = 1e-05
        key = jax.random.key(seed)
        ks = jax.random.split(key, 9)
        s = 0.02
        return {'x': jax.random.normal(ks[0], (B, S, D), dtype=jnp.float32), 'W1': jax.random.normal(ks[1], (E, D, H), dtype=jnp.float32) * s, 'b1': jnp.zeros((E, H), dtype=jnp.float32), 'W2': jax.random.normal(ks[2], (E, H, DO), dtype=jnp.float32) * s, 'b2': jnp.zeros((E, DO), dtype=jnp.float32), 'gate_W': jax.random.normal(ks[3], (D, E), dtype=jnp.float32) * s, 'shared_W': jax.random.normal(ks[4], (D, DO), dtype=jnp.float32) * s, 'shared_b': jnp.zeros((DO,), dtype=jnp.float32), 'gamma': jnp.ones((DO,), dtype=jnp.float32), 'beta': jnp.zeros((DO,), dtype=jnp.float32)}
    _L1_ffn_in = _L1_ffn_setup()
    _d = {'L0_attn_X': _L0_attn_in['X'], 'L0_attn_Wq': _L0_attn_in['Wq'], 'L0_attn_Wk': _L0_attn_in['Wk'], 'L0_attn_Wv': _L0_attn_in['Wv'], 'L0_attn_Wo': _L0_attn_in['Wo'], 'L0_ffn_Wg': _L0_ffn_in['Wg'], 'L0_ffn_bg': _L0_ffn_in['bg'], 'L0_ffn_W0': _L0_ffn_in['W0'], 'L0_ffn_b0': _L0_ffn_in['b0'], 'L0_ffn_W1': _L0_ffn_in['W1'], 'L0_ffn_b1': _L0_ffn_in['b1'], 'L0_ffn_W2': _L0_ffn_in['W2'], 'L0_ffn_b2': _L0_ffn_in['b2'], 'L1_attn_w': _L1_attn_in['w'], 'L1_attn_u': _L1_attn_in['u'], 'L1_attn_rk': _L1_attn_in['rk'], 'L1_attn_rv': _L1_attn_in['rv'], 'L1_attn_rr': _L1_attn_in['rr'], 'L1_attn_crk': _L1_attn_in['crk'], 'L1_attn_crr': _L1_attn_in['crr'], 'L1_attn_Wk': _L1_attn_in['Wk'], 'L1_attn_Wv': _L1_attn_in['Wv'], 'L1_attn_Wr': _L1_attn_in['Wr'], 'L1_attn_Wck': _L1_attn_in['Wck'], 'L1_attn_Wcv': _L1_attn_in['Wcv'], 'L1_attn_Wcr': _L1_attn_in['Wcr'], 'L1_attn_ln1_g': _L1_attn_in['ln1_g'], 'L1_attn_ln1_b': _L1_attn_in['ln1_b'], 'L1_attn_ln2_g': _L1_attn_in['ln2_g'], 'L1_attn_ln2_b': _L1_attn_in['ln2_b'], 'L1_ffn_W1': _L1_ffn_in['W1'], 'L1_ffn_b1': _L1_ffn_in['b1'], 'L1_ffn_W2': _L1_ffn_in['W2'], 'L1_ffn_b2': _L1_ffn_in['b2'], 'L1_ffn_gate_W': _L1_ffn_in['gate_W'], 'L1_ffn_shared_W': _L1_ffn_in['shared_W'], 'L1_ffn_shared_b': _L1_ffn_in['shared_b'], 'L1_ffn_gamma': _L1_ffn_in['gamma'], 'L1_ffn_beta': _L1_ffn_in['beta']}
    _x0 = _d['L0_attn_X']
    _d['L0_attn_X'] = jax.random.normal(jax.random.fold_in(jax.random.key(seed), 1), (8, 256, 128), dtype=_x0.dtype)
    del _x0
    return _d

def reference(L0_attn_X, L0_attn_Wq, L0_attn_Wk, L0_attn_Wv, L0_attn_Wo, L0_ffn_Wg, L0_ffn_bg, L0_ffn_W0, L0_ffn_b0, L0_ffn_W1, L0_ffn_b1, L0_ffn_W2, L0_ffn_b2, L1_attn_w, L1_attn_u, L1_attn_rk, L1_attn_rv, L1_attn_rr, L1_attn_crk, L1_attn_crr, L1_attn_Wk, L1_attn_Wv, L1_attn_Wr, L1_attn_Wck, L1_attn_Wcv, L1_attn_Wcr, L1_attn_ln1_g, L1_attn_ln1_b, L1_attn_ln2_g, L1_attn_ln2_b, L1_ffn_W1, L1_ffn_b1, L1_ffn_W2, L1_ffn_b2, L1_ffn_gate_W, L1_ffn_shared_W, L1_ffn_shared_b, L1_ffn_gamma, L1_ffn_beta):

    def _L0_attn_ref(X, Wq, Wk, Wv, Wo):
        import jax, jax.numpy as jnp
        import numpy as np
        D_MODEL = 128
        N_HEADS = 16
        N_KV_HEADS = 4
        HEAD_DIM = 64
        S = 4
        W = 32
        B = 2
        T = 256

        def _sink_mask(seq_len, sink, window):
            t = jnp.arange(seq_len)
            i = t[:, None]
            j = t[None, :]
            sink_band = j < min(sink, seq_len)
            window_band = j >= jnp.maximum(i - window + 1, 0)
            causal = j <= i
            return causal & (sink_band | window_band)
        b, t, _ = X.shape
        d = HEAD_DIM
        Q = (X @ Wq).reshape(b, t, N_HEADS, d)
        K = (X @ Wk).reshape(b, t, N_KV_HEADS, d)
        V = (X @ Wv).reshape(b, t, N_KV_HEADS, d)
        rep = N_HEADS // N_KV_HEADS
        K = jnp.repeat(K, rep, axis=2)
        V = jnp.repeat(V, rep, axis=2)
        scale = 1.0 / np.sqrt(d)
        logits = jnp.einsum('bthd,bshd->bhts', Q * scale, K)
        M = _sink_mask(t, S, W)[None, None]
        neg = jnp.finfo(logits.dtype).min
        masked = jnp.where(M, logits, neg)
        mx = jnp.max(masked, axis=-1, keepdims=True)
        exp = jnp.exp(masked - mx) * M.astype(logits.dtype)
        denom = jnp.maximum(jnp.sum(exp, axis=-1, keepdims=True), jnp.finfo(logits.dtype).tiny)
        P = exp / denom
        Y = jnp.einsum('bhts,bshd->bthd', P, V)
        return Y.reshape(b, t, N_HEADS * d) @ Wo

    def _L0_ffn_ref(x, Wg, bg, W0, b0, W1, b1, W2, b2):
        import jax, jax.numpy as jnp
        import numpy as np
        NUM_EXPERTS = 8
        TOP_K = 2
        D_MODEL = 128
        D_HID = 512
        BATCH, SEQ = (2, 256)
        n, s, d = x.shape
        gate_logits = x @ Wg + bg
        top_vals, top_idx = jax.lax.top_k(gate_logits, TOP_K)
        w = jax.nn.softmax(top_vals, axis=-1)
        combine = jnp.sum(jax.nn.one_hot(top_idx, NUM_EXPERTS, dtype=x.dtype) * w[..., None], axis=-2)
        xf = x.reshape(n * s, d)
        h = jnp.einsum('td,edh->eth', xf, W0) + b0[:, None, :]
        g = jax.nn.silu(jnp.einsum('td,edh->eth', xf, W1) + b1[:, None, :])
        y = jnp.einsum('eth,ehd->etd', h * g, W2) + b2[:, None, :]
        out = jnp.einsum('te,etd->td', combine.reshape(n * s, NUM_EXPERTS), y)
        return out.reshape(n, s, d)

    def _L1_attn_ref(x, w, u, rk, rv, rr, crk, crr, Wk, Wv, Wr, Wck, Wcv, Wcr, ln1_g, ln1_b, ln2_g, ln2_b):
        import jax, jax.numpy as jnp
        import numpy as np
        B, T, C = (8, 512, 128)
        LN_EPS = 1e-05
        NEG_INF = -1e+38

        def _ln(x, g, b):
            mu = jnp.mean(x, axis=-1, keepdims=True)
            var = jnp.mean(jnp.square(x - mu), axis=-1, keepdims=True)
            return (x - mu) * jax.lax.rsqrt(var + LN_EPS) * g + b

        def _shift(x):
            return jnp.concatenate([jnp.zeros_like(x[:, :1]), x[:, :-1]], axis=1)

        def _wkv(w, u, k, v):
            kt = jnp.moveaxis(k, 1, 0)
            vt = jnp.moveaxis(v, 1, 0)
            aa = jnp.zeros(k.shape[::2], k.dtype)
            bb = jnp.zeros(k.shape[::2], k.dtype)
            pp = jnp.full(k.shape[::2], NEG_INF, k.dtype)

            def step(carry, kv):
                aa, bb, pp = carry
                kk, vv = kv
                p = jnp.maximum(pp, u + kk)
                e1 = jnp.exp(pp - p)
                e2 = jnp.exp(u + kk - p)
                y = (e1 * aa + e2 * vv) / (e1 + e2)
                p2 = jnp.maximum(pp + w, w + kk)
                e1u = jnp.exp(pp + w - p2)
                e2u = jnp.exp(w + kk - p2)
                aa = e1u * aa + e2u * vv
                bb = e1u + e2u
                pp = p2 + jnp.log(bb)
                return ((aa, bb, pp), y)
            _, ys = jax.lax.scan(step, (aa, bb, pp), (kt, vt))
            return jnp.moveaxis(ys, 0, 1)
        xa = _ln(x, ln1_g, ln1_b)
        xp = _shift(xa)
        xk = xa * rk + xp * (1.0 - rk)
        xv = xa * rv + xp * (1.0 - rv)
        xr = xa * rr + xp * (1.0 - rr)
        k = jnp.einsum('btc,dc->btd', xk, Wk)
        v = jnp.einsum('btc,dc->btd', xv, Wv)
        r = jnp.einsum('btc,dc->btd', xr, Wr)
        wkv = _wkv(w, u, k, v)
        x1 = x + jax.nn.sigmoid(r) * wkv
        xb = _ln(x1, ln2_g, ln2_b)
        xpb = _shift(xb)
        xck = xb * crk + xpb * (1.0 - crk)
        xcr = xb * crr + xpb * (1.0 - crr)
        kc = jnp.square(jax.nn.relu(jnp.einsum('btc,dc->btd', xck, Wck)))
        vc = jnp.einsum('bth,dh->btd', kc, Wcv)
        out = x1 + jax.nn.sigmoid(jnp.einsum('btc,dc->btd', xcr, Wcr)) * vc
        return out

    def _L1_ffn_ref(x, W1, b1, W2, b2, gate_W, shared_W, shared_b, gamma, beta):
        import jax, jax.numpy as jnp
        import numpy as np
        B, S, D, E, H, DO = (4, 256, 128, 8, 512, 128)
        TOP_K = 2
        LN_EPS = 1e-05
        d = x.shape[-1]
        flat = x.reshape(-1, d)
        n_exp = gate_W.shape[-1]
        probs = jax.nn.softmax(flat @ gate_W, axis=-1)
        topk_w, topk_idx = jax.lax.top_k(probs, TOP_K)
        topk_w = topk_w / topk_w.sum(axis=-1, keepdims=True)
        combine = (jax.nn.one_hot(topk_idx, n_exp, dtype=flat.dtype) * topk_w[..., None]).sum(axis=1)
        out = 0.5 * jax.nn.gelu(flat @ shared_W + shared_b, approximate=False)
        for e in range(n_exp):
            h = jax.nn.gelu(flat @ W1[e] + b1[e], approximate=False)
            out = out + combine[:, e:e + 1] * (h @ W2[e] + b2[e])
        mean = out.mean(axis=-1, keepdims=True)
        var = ((out - mean) ** 2).mean(axis=-1, keepdims=True)
        out = (out - mean) * jax.lax.rsqrt(var + LN_EPS) * gamma + beta
        return out.reshape(*x.shape[:-1], out.shape[-1])
    x = L0_attn_X
    x = x + 0.5 * _L0_ffn_ref(_layernorm(x, axis=-1), L0_ffn_Wg, L0_ffn_bg, L0_ffn_W0, L0_ffn_b0, L0_ffn_W1, L0_ffn_b1, L0_ffn_W2, L0_ffn_b2)
    x = x + _L0_attn_ref(_layernorm(x, axis=-1), L0_attn_Wq, L0_attn_Wk, L0_attn_Wv, L0_attn_Wo)
    x = x + 0.5 * _L0_ffn_ref(_layernorm(x, axis=-1), L0_ffn_Wg, L0_ffn_bg, L0_ffn_W0, L0_ffn_b0, L0_ffn_W1, L0_ffn_b1, L0_ffn_W2, L0_ffn_b2)
    x = x + 0.5 * _L1_ffn_ref(_layernorm(x, axis=-1), L1_ffn_W1, L1_ffn_b1, L1_ffn_W2, L1_ffn_b2, L1_ffn_gate_W, L1_ffn_shared_W, L1_ffn_shared_b, L1_ffn_gamma, L1_ffn_beta)
    x = x + _L1_attn_ref(_layernorm(x, axis=-1), L1_attn_w, L1_attn_u, L1_attn_rk, L1_attn_rv, L1_attn_rr, L1_attn_crk, L1_attn_crr, L1_attn_Wk, L1_attn_Wv, L1_attn_Wr, L1_attn_Wck, L1_attn_Wcv, L1_attn_Wcr, L1_attn_ln1_g, L1_attn_ln1_b, L1_attn_ln2_g, L1_attn_ln2_b)
    x = x + 0.5 * _L1_ffn_ref(_layernorm(x, axis=-1), L1_ffn_W1, L1_ffn_b1, L1_ffn_W2, L1_ffn_b2, L1_ffn_gate_W, L1_ffn_shared_W, L1_ffn_shared_b, L1_ffn_gamma, L1_ffn_beta)
    return x

_drawn_inputs = setup_inputs


def setup_inputs(seed=0):
    import zlib

    import numpy as np

    out = dict(_drawn_inputs(seed))
    spreads = {'L0_ffn_bg': (0.0, 0.1),
     'L0_ffn_b0': (0.0, 0.333),
     'L0_ffn_b1': (0.0, 0.1),
     'L0_ffn_b2': (0.0, 0.1),
     'L1_attn_ln1_g': (1.0, 0.2),
     'L1_attn_ln1_b': (0.0, 0.1),
     'L1_attn_ln2_g': (1.0, 0.6),
     'L1_attn_ln2_b': (0.0, 0.8),
     'L1_ffn_b1': (0.0, 0.1),
     'L1_ffn_b2': (0.0, 0.1),
     'L1_ffn_shared_b': (0.0, 0.1),
     'L1_ffn_gamma': (1.0, 0.2),
     'L1_ffn_beta': (0.0, 0.1)}
    factors = {'L0_attn_Wq': 2.934,
     'L0_attn_Wk': 3.5,
     'L1_attn_w': 3.759,
     'L1_attn_u': 64.0,
     'L1_attn_rk': 4.862,
     'L1_attn_rv': 4.073,
     'L1_attn_rr': 4.351,
     'L1_attn_crk': 7.741,
     'L1_attn_crr': 8.0,
     'L1_attn_Wk': 3.881,
     'L1_attn_Wr': 3.5,
     'L1_attn_Wck': 6.738,
     'L1_attn_Wcv': 5.531,
     'L1_attn_Wcr': 8.0}
    for name, (base, spread) in spreads.items():
        noise = np.random.default_rng([zlib.crc32(name.encode()), seed]).standard_normal(out[name].shape)
        drawn = base * np.exp(spread * noise) if base else spread * noise
        out[name] = jnp.asarray(drawn.astype(out[name].dtype))
    for name, factor in factors.items():
        out[name] = (out[name] * factor).astype(out[name].dtype)
    return out
```

```python
import concourse.bass as bass
from concourse import mybir
from contextlib import ExitStack

F32 = mybir.dt.float32
R32 = mybir.dt.float32r
U32 = mybir.dt.uint32
ALU = mybir.AluOpType
ACT = mybir.ActivationFunctionType
AX = mybir.AxisListType

P = 128
B, T, D = 8, 256, 128
NT = B * T // P
NBLK = 4
TPB = NT // NBLK
BC = TPB * P
E = 8
HC = 4
EPS = 1e-5
AHEAD = 3

GLU_COLS = 3 * 512 + 2 * HC + 1
MLP_COLS = 2 * 512 + HC + 1

HD, KVH = 64, 4
QW, SINK = 32, 4
QC = T // QW
KEYS = 2 * QW + SINK
PAD = QW
ATTN_COLS = 1024 + 256 + 256 + 1024
QCOL, KCOL, VCOL, OCOL = 0, 1024, 1280, 1536
MASKED = -3.0e38
TINY = 1.1754943508222875e-38


KW, VW, RW, CKW, CRW, CVW, RWKV_COLS = 0, 128, 256, 384, 896, 1024, 1536
C_W, C_U, C_RK, C_RV, C_RR, C_CRK, C_CRR, C_G1, C_B1, C_G2, C_B2, N_COLS = range(12)
NEG_INF = -1e38


class Moe:

    def __init__(self, name, gated):
        self.name, self.gated = name, gated
        self.ups = 2 if gated else 1
        self.cols = GLU_COLS if gated else MLP_COLS
        self.wcols = (self.ups + 1) * 512
        self.bias_lin = self.wcols
        self.bias_act = self.wcols + HC * (self.ups - 1)
        self.bias_out = self.bias_act + HC
        self.combine_scale = 0.5 if gated else 1.0
        self.func = ACT.Silu if gated else ACT.Gelu


def signals_of_one_use(kind, what):
    chunks, units = E * NBLK * HC, E * NBLK
    pieces = 3 if kind == "glu" else 2
    return {"_up": chunks, "_act": chunks, "_hid": chunks, "_hi": chunks, "_lo": chunks, "_down": chunks,
            "_scaled": units, "_acc": units, "_wh": pieces * E, "_w_ready": pieces * E,
            "_raw_in0": 16 * E // 2, "_raw_in1": 16 * E // 2, "_comb_in0": 16 * E // 2, "_comb_in1": 16 * E // 2,
            "_comb_out": 16 * NBLK, "_acc_init": 1 if kind == "glu" else NBLK}.get(what, NBLK)


class Stage:

    def __init__(self, kind, use):
        self.kind, self.use = kind, use

    def __add__(self, what):
        return self.kind + what

    def at(self, what, value):
        return value + self.use * signals_of_one_use(self.kind, what) if self.use else value


def later(value):
    return not isinstance(value, int) or value > 0


def build_program(nc, x_in, glu_pack, glu_gate, glu_gate_b, mlp_pack, mlp_gate, mlp_shared, mlp_rows,
                  attn_pack, rwkv_pack, rwkv_cols, out, stages=("glu", "attn", "glu", "mlp", "rwkv", "mlp")):
    ctx = ExitStack()
    with ctx:
        def sb(name, shape, dt=F32):
            return ctx.enter_context(nc.sbuf_tensor(name, shape, dt))

        sems = {}

        def sem(name):
            if name not in sems:
                sems[name] = ctx.enter_context(nc.semaphore(name))
            return sems[name]

        x_tok = sb("x_tok", [P, NT, D])
        ident = sb("ident", [P, P])
        iota8 = sb("iota8", [P, E])
        one = sb("one", [P, 1])
        neghalf = sb("neghalf", [P, TPB])
        stats = sb("stats", [P, TPB, 6])
        meanvar = sb("meanvar", [P, TPB, 2])
        var_eps = sb("var_eps", [P, TPB])
        rstd = sb("rstd", [P, TPB])
        xn_tok = sb("xn_tok", [P, TPB, D])
        comb_dram = nc.dram_tensor("comb_scratch", [NBLK, E, BC], F32)

        banks = [ctx.enter_context(nc.psum_tensor(f"bank{i}", [P, 512], F32)) for i in range(8)]
        UP_ACT, UP_LIN, DOWN = banks[0:2], banks[2:4], banks[4:6]
        TR, MISC = banks[6], banks[7]

        moe_ctx = ctx
        raw = sb("raw_weights", [P, 2, GLU_COLS])
        wh = sb("weights_hi", [P, 2, 1536], R32)
        wl = sb("weights_lo", [P, 2, 1536], R32)
        gate_raw = {"glu": sb("glu_gate_raw", [P, E]), "mlp": sb("mlp_gate_raw", [P, E])}
        gate_h = {n: sb(n + "_gate_hi", [P, E], R32) for n in ("glu", "mlp")}
        gate_l = {n: sb(n + "_gate_lo", [P, E], R32) for n in ("glu", "mlp")}
        gate_bias = sb("gate_bias", [P, E])
        shared_raw = sb("shared_raw", [P, D + 1])
        shared_h = sb("shared_hi", [P, D], R32)
        shared_l = sb("shared_lo", [P, D], R32)
        half_gamma = sb("half_gamma", [P, D])
        half_beta = sb("half_beta", [P, D])
        logits = sb("logits", [P, TPB, E])
        top = sb("top", [P, TPB, 8])
        top_at = sb("top_at", [P, TPB, 8], U32)
        top_atf = sb("top_atf", [P, TPB, 2])
        gap = sb("gap", [P, TPB])
        tanh_gap = sb("tanh_gap", [P, TPB])
        w_first = sb("w_first", [P, TPB])
        w_second = sb("w_second", [P, TPB])
        pick1 = sb("pick1", [P, E, TPB])
        pick2 = sb("pick2", [P, E, TPB])
        comb = sb("comb", [P, E, TPB])
        comb_rows = sb("comb_rows", [E * TPB, P])
        acc = sb("acc", [P, NBLK, BC])
        mask = sb("mask", [P, 3, KEYS])

        def shared_place(*tensors):
            with ExitStack() as place:
                return [place.enter_context(nc.sbuf_tensor(n, s, d)) for n, s, d in tensors]

        xh, xl, comb_bc, act_ring, hid, hid_h, hid_l, scaled = shared_place(
            ("xh", [P, NBLK, BC], R32), ("xl", [P, NBLK, BC], R32),
            ("comb_bc", [P, 2, NBLK, BC], F32), ("act_ring", [P, 2, BC], F32), ("hid", [P, 4, BC], F32),
            ("hid_hi", [P, 4, BC], R32), ("hid_lo", [P, 4, BC], R32), ("scaled", [P, 2, BC], F32))
        (attn_raw, ah, al, xa_h, xa_l, win_h, win_l, q_sb, k_sb, v_sb, yh, yl, scores, probs, probsT, rowmax, rowsum,
         rowinv) = shared_place(
            ("attn_raw", [P, ATTN_COLS], F32), ("attn_hi", [P, ATTN_COLS], R32), ("attn_lo", [P, ATTN_COLS], R32),
            ("xa_hi", [P, 2, PAD + T], R32), ("xa_lo", [P, 2, PAD + T], R32),
            ("win_hi", [P, 2, QC, KEYS], R32), ("win_lo", [P, 2, QC, KEYS], R32),
            ("q_sb", [P, 2 * QC, 2, 4, QW], F32), ("k_sb", [P, 2, 2, QC, 2, KEYS], F32),
            ("v_sb", [KEYS, 2 * QC, KVH * HD], F32), ("y_hi", [P, 8, BC], R32), ("y_lo", [P, 8, BC], R32),
            ("scores", [P, 2, KVH, KEYS], F32), ("probs", [P, 4, KVH, KEYS], F32), ("probsT", [KEYS, 2, KVH * P], F32),
            ("rowmax", [P, KVH], F32), ("rowsum", [P, 4, KVH], F32), ("rowinv", [P, 4, KVH], F32))

        (mix_raw, mix_cols, one_minus, mix_f, mix_h, mix_l, cv_h, cv_l, xs_h, xs_l, xin, xf, kf, vf, sr, mm, pp, aa,
         t1, t2, ss, gap_kp, q_mix, zf, relu, kc, kc_h, kc_l, sig_c, out_c) = shared_place(
            ("mix_raw", [P, RWKV_COLS], F32), ("mix_cols", [P, N_COLS], F32), ("one_minus", [P, 5], F32),
            ("mix_f", [P, 1024], F32), ("mix_hi", [P, 2, 1024], R32), ("mix_lo", [P, 2, 1024], R32),
            ("cv_hi", [P, 512], R32), ("cv_lo", [P, 512], R32),
            ("xs_hi", [P, B, T + 1], R32), ("xs_lo", [P, B, T + 1], R32), ("xin", [P, NT, D], F32),
            ("xf", [P, 2, T], F32), ("kf", [P, B, T], F32), ("vf", [P, B, T], F32), ("sr", [P, B, T], F32),
            ("mm", [P, 2, T + 1], F32), ("pp", [P, 2, T + 1], F32), ("aa", [P, 2, T + 1], F32),
            ("t1", [P, 2, T], F32), ("t2", [P, 2, T], F32), ("ss", [P, 2, T], F32), ("gap_kp", [P, B, T], F32),
            ("q_mix", [P, 2, T], F32), ("zf", [P, B, T], F32), ("relu", [P, 2, BC], F32), ("kc", [P, 2, BC], F32),
            ("kc_hi", [P, 2, BC], R32), ("kc_lo", [P, 2, BC], R32), ("sig_c", [P, BC], F32), ("out_c", [P, BC], F32))
        y_mix = kf

        order = [(Stage(kind, stages[:n].count(kind)), kind) for n, kind in enumerate(stages)]

        def x_done(n):
            return sem("x_loaded") if n < 0 else sem(order[n][0] + "_x_done")

        def x_at(n, blocks):
            return 16 * NBLK if n < 0 else order[n][0].at("_x_done", blocks)

        chain = [0]

        def link(ins):
            chain[0] += 1
            ins.then_inc(sem("dve_chain"), 1)
            nc.vector.wait_ge(sem("dve_chain"), chain[0])

        block = ctx.enter_context(nc.Block())

        def moe_load(sp, n, st, m, e, par):
            pack = glu_pack if m.gated else mlp_pack
            if later(4 * (e - 1)):
                sp.wait_ge(sem(st + "_scaled"), st.at("_scaled", 4 * (e - 1)))
            sp.dma_start(raw[:, par, 0:m.cols], pack[:, bass.ds(e * m.cols, m.cols)]).then_inc(
                sem(st + f"_raw_in{par}"), 16)

        def moe_load_comb(sp, n, st, m, e, par):
            src = comb_dram.ap()[:, bass.ds(e, 1), :]
            src = src.rearrange("b e n -> e b n").broadcast_to([P, NBLK, BC])
            sp.dma_start(comb_bc[:, par, :, :], src).then_inc(sem(st + f"_comb_in{par}"), 16)

        def moe_sp(sp, n, st, m):
            old = [order[i][0] for i in range(n) if stages[i] in ("glu", "mlp")]
            if old:
                sp.wait_ge(sem(old[-1] + "_scaled"), old[-1].at("_scaled", NBLK * E))
            moe_load(sp, n, st, m, 0, 0)
            moe_load(sp, n, st, m, 1, 1)
            for b in range(NBLK):
                sp.wait_ge(sem(st + "_comb_rows"), st.at("_comb_rows", b + 1))
                sp.dma_start(comb_dram.ap()[b, :, :].rearrange("e (t p) -> (e t) p", p=P), comb_rows[:, :]).then_inc(
                    sem(st + "_comb_out"), 16)
            sp.wait_ge(sem(st + "_comb_out"), st.at("_comb_out", 16 * NBLK))
            moe_load_comb(sp, n, st, m, 0, 0)
            moe_load_comb(sp, n, st, m, 1, 1)
            with sp.Fori(0, E // 2 - 1) as i:
                for par in range(2):
                    sp.wait_ge(sem(st + "_scaled"), st.at("_scaled", 8 * i + 4 * (par + 1)))
                    sp.dma_start(raw[:, par, 0:m.cols],
                                 (glu_pack if m.gated else mlp_pack)[:, bass.ds((2 * i + par + 2) * m.cols, m.cols)]
                                 ).then_inc(sem(st + f"_raw_in{par}"), 16)
                    moe_load_comb(sp, n, st, m, 2 * i + par + 2, par)

        def split(pool, dst_h, dst_l, src, done):
            pool.tensor_copy(dst_h, src).then_inc(done, 1)

        def moe_split_piece(pool, st, m, count, slot, piece):
            cols = slice(piece * 512, piece * 512 + 512)
            pool.tensor_tensor(wh[:, slot, cols], raw[:, slot, cols], one[:, :].broadcast_to([P, 512]),
                               ALU.mult).then_inc(sem(st + "_wh"), 1)
            pool.wait_ge(sem(st + "_wh"), st.at("_wh", count + 1))
            pool.tensor_tensor(wl[:, slot, cols], raw[:, slot, cols], wh[:, slot, cols].bitcast(F32),
                               ALU.subtract).then_inc(sem(st + "_w_ready"), 1)

        def rstd_pool(pool, st, name, n):
            pool.wait_ge(sem(st + name + "_var"), st.at(name + "_var", n + 1))
            pool.tensor_tensor(rstd[:, :], var_eps[:, :], neghalf[:, :], ALU.pow).then_inc(sem(st + name + "_rstd"), 1)

        def moe_pool(pool, n, st, m):
            pieces = m.ups + 1
            pool.wait_ge(sem(st + "_raw_in0"), st.at("_raw_in0", 16))
            old = [order[i][0] for i in range(n) if stages[i] in ("glu", "mlp")]
            if old:
                pool.wait_ge(sem(old[-1] + "_down"), old[-1].at("_down", HC * NBLK * E))
            for c in range(pieces):
                moe_split_piece(pool, st, m, c, 0, c)
            for b in range(NBLK):
                rstd_pool(pool, st, "_in", b)
            if m.gated:
                pool.memset(acc[:, :, :], 0.0).then_inc(sem(st + "_acc_init"), 1)
                pool.wait_ge(sem(st + "_acc_init"), st.at("_acc_init", 1))
            else:
                pool.wait_ge(sem(st + "_acc_init"), st.at("_acc_init", NBLK))

            def expert(e, par, last, next_load=None):
                for b in range(NBLK):
                    u = NBLK * e + b
                    pool.wait_ge(sem(st + "_scaled"), st.at("_scaled", u + 1))
                    if later(u):
                        pool.wait_ge(sem(st + "_acc"), st.at("_acc", u))
                    pool.tensor_tensor(acc[:, b, :], acc[:, b, :], scaled[:, b % 2, :],
                                       ALU.add).then_inc(sem(st + "_acc"), 1)
                    if last:
                        continue
                    if b == 0:
                        pool.wait_ge(sem(st + f"_raw_in{1 - par}"), st.at(f"_raw_in{1 - par}", next_load))
                    for piece in ((0, 1), (2,), (), ())[b][:pieces]:
                        if piece < pieces:
                            moe_split_piece(pool, st, m, pieces * (e + 1) + piece, 1 - par, piece)

            expert(0, 0, False, 16)
            with pool.Fori(0, E // 2 - 1) as i:
                expert(2 * i + 1, 1, False, 16 * i + 32)
                expert(2 * i + 2, 0, False, 16 * i + 32)
            expert(E - 1, 1, True)
            if not m.gated:
                for b in range(NBLK):
                    rstd_pool(pool, st, "_out", b)

        def moe_act(act, n, st, m):
            for b in range(NBLK):
                act.wait_ge(sem(st + "_xT"), st.at("_xT", b + 1))
                act.activation(xh[:, b, :], TR[:, :], ACT.Copy).then_inc(sem(st + "_xh"), 1)
                if not m.gated:
                    act.wait_ge(sem(st + "_shared"), st.at("_shared", b + 1))
                    act.activation(acc[:, b, :], UP_LIN[0][:, :], ACT.Gelu,
                                   bias=shared_raw[:, D:D + 1]).then_inc(sem(st + "_shared_act"), 1)
                act.wait_ge(sem(st + "_gap"), st.at("_gap", b + 1))
                act.activation(tanh_gap[:, :], gap[:, :], ACT.Tanh, scale=0.5).then_inc(sem(st + "_tanh"), 1)
                act.wait_ge(sem(st + "_combT"), st.at("_combT", b + 1))
                if b:
                    act.wait_ge(sem(st + "_comb_out"), st.at("_comb_out", 16 * b))
                act.activation(comb_rows[:, :], MISC[0:E * TPB, 128:256], ACT.Copy).then_inc(
                    sem(st + "_comb_rows"), 1)

            def first(e, par, c16):
                k = 16 * e + c16
                c = c16 % HC
                act.wait_ge(sem(st + "_up"), st.at("_up", k + 1))
                dst = act_ring[:, k16(c16) % 2, :] if m.gated else hid[:, c16 % 4, :]
                if not m.gated:
                    if later(k - 3):
                        act.wait_ge(sem(st + "_lo"), st.at("_lo", k - 3))
                act.activation(dst, UP_ACT[c16 % 2][:, :], m.func,
                               bias=raw[:, par, m.bias_act + c:m.bias_act + c + 1]).then_inc(sem(st + "_act"), 1)

            def k16(c16):
                return c16

            def second(e, c16):
                k = 16 * e + c16
                act.wait_ge(sem(st + ("_hid" if m.gated else "_act")), st.at(("_hid" if m.gated else "_act"), k + 1))
                if later(k - 3):
                    act.wait_ge(sem(st + "_down"), st.at("_down", k - 3))
                act.activation(hid_h[:, c16 % 4, :], hid[:, c16 % 4, :], ACT.Copy).then_inc(sem(st + "_hi"), 1)

            def expert(e, par, last):
                for c16 in range(16):
                    if c16 < 15:
                        first(e, par, c16 + 1)
                    elif not last:
                        first(e + 1, 1 - par, 0)
                    if m.gated:
                        second(e, c16)

            first(0, 0, 0)
            expert(0, 0, False)
            with act.Fori(0, E // 2 - 1) as i:
                expert(2 * i + 1, 1, False)
                expert(2 * i + 2, 0, False)
            expert(E - 1, 1, True)

        def three(pe, dst, w_h, w_l, v_h, v_l, start=True, stop=True):
            nc.tensor.matmul(dst, w_h, v_h, start=start, stop=False)
            nc.tensor.matmul(dst, w_h, v_l, start=False, stop=False)
            return nc.tensor.matmul(dst, w_l, v_h, start=False, stop=stop)

        def moe_pe(pe, n, st, m):
            g = "glu" if m.gated else "mlp"
            for b in range(NBLK):
                pe.wait_ge(sem(st + "_in_norm"), st.at("_in_norm", b + 1))
                if b:
                    pe.wait_ge(sem(st + "_xl"), st.at("_xl", b))
                elif n:
                    pe.wait_ge(x_done(n - 1), x_at(n - 1, NBLK))
                for t in range(TPB):
                    ins = nc.tensor.transpose(TR[:, t * P:(t + 1) * P], xn_tok[:, t, :], ident[:, :])
                ins.then_inc(sem(st + "_xT"), 1)
                pe.wait_ge(sem(st + "_xl"), st.at("_xl", b + 1))
                if b == 0:
                    pe.wait_ge(sem("const_ready"), 1)
                if not m.gated:
                    if b:
                        pe.wait_ge(sem(st + "_shared_act"), st.at("_shared_act", b))
                    three(pe, UP_LIN[0][:, :], shared_h[:, :], shared_l[:, :], xh[:, b, :], xl[:, b, :]).then_inc(
                        sem(st + "_shared"), 1)
                if b:
                    pe.wait_ge(sem(st + "_comb_rows"), st.at("_comb_rows", b))
                for t in range(TPB):
                    tok = slice(t * P, (t + 1) * P)
                    ins = three(pe, MISC[:, t * E:(t + 1) * E], xh[:, b, tok], xl[:, b, tok], gate_h[g][:, :],
                                gate_l[g][:, :])
                ins.then_inc(sem(st + "_logits"), 1)
                pe.wait_ge(sem(st + "_comb"), st.at("_comb", b + 1))
                nc.tensor.transpose(MISC[0:E * TPB, 128:256], comb[:, :, :].rearrange("p e t -> p (e t)"),
                                    ident[:, :]).then_inc(sem(st + "_combT"), 1)

            def up(e, par, c16):
                k = 16 * e + c16
                b, c = c16 // HC, c16 % HC
                if c16 == 0:
                    pe.wait_ge(sem(st + "_w_ready"), st.at("_w_ready", (m.ups + 1) * (e + 1)))
                if later(k - 1):
                    pe.wait_ge(sem(st + ("_hid" if m.gated else "_act")), st.at(("_hid" if m.gated else "_act"), k - 1))
                if m.gated:
                    cols = slice(c * P, c * P + P)
                    three(pe, UP_LIN[c16 % 2][:, :], wh[:, par, cols], wl[:, par, cols], xh[:, b, :], xl[:, b, :])
                o = (m.ups - 1) * 512
                cols = slice(o + c * P, o + c * P + P)
                three(pe, UP_ACT[c16 % 2][:, :], wh[:, par, cols], wl[:, par, cols], xh[:, b, :],
                      xl[:, b, :]).then_inc(sem(st + "_up"), 1)

            def down(e, par, c16):
                k = 16 * e + c16
                b, c = c16 // HC, c16 % HC
                pe.wait_ge(sem(st + "_lo"), st.at("_lo", k + 1))
                if c == 0:
                    if later(NBLK * e + b - 1):
                        pe.wait_ge(sem(st + "_scaled"), st.at("_scaled", NBLK * e + b - 1))
                o = m.ups * 512 + c * P
                three(pe, DOWN[b % 2][:, :], wh[:, par, o:o + P], wl[:, par, o:o + P], hid_h[:, c16 % 4, :],
                      hid_l[:, c16 % 4, :], start=c == 0, stop=c == HC - 1).then_inc(sem(st + "_down"), 1)

            def expert(e, par, last):
                for c16 in range(16):
                    if c16 < 16 - AHEAD:
                        up(e, par, c16 + AHEAD)
                    elif not last:
                        up(e + 1, 1 - par, c16 - (16 - AHEAD))
                    down(e, par, c16)

            for c16 in range(AHEAD):
                up(0, 0, c16)
            expert(0, 0, False)
            with pe.Fori(0, E // 2 - 1) as i:
                expert(2 * i + 1, 1, False)
                expert(2 * i + 2, 0, False)
            expert(E - 1, 1, True)
            for b in range(NBLK):
                pe.wait_ge(sem(st + "_acc"), st.at("_acc", NBLK * (E - 1) + b + 1))
                if b:
                    pe.wait_ge(sem(st + "_outT_read"), st.at("_outT_read", b))
                for t in range(TPB):
                    ins = nc.tensor.transpose(TR[:, t * P:(t + 1) * P], acc[:, b, t * P:(t + 1) * P], ident[:, :])
                ins.then_inc(sem(st + "_outT"), 1)

        def layernorm(v, st, name, src, n, dst=None):
            for t in range(TPB):
                ins = nc.vector.bn_stats(stats[:, t, :], src(t))
            link(ins)
            for t in range(TPB):
                ins = nc.vector.bn_aggr(meanvar[:, t, :], stats[:, t, :])
            link(ins)
            nc.vector.tensor_scalar_add(var_eps[:, :], meanvar[:, :, 1], EPS).then_inc(sem(st + name + "_var"), 1)
            v.wait_ge(sem(st + name + "_rstd"), st.at(name + "_rstd", n + 1))
            dst = dst or (lambda t: xn_tok[:, t, :])
            for t in range(TPB):
                ins = nc.vector.tensor_scalar(dst(t), src(t), meanvar[:, t, 0:1], rstd[:, t:t + 1],
                                              ALU.subtract, ALU.mult)
            return ins

        def moe_dve(v, n, st, m):
            for b in range(NBLK):
                v.wait_ge(x_done(n - 1), x_at(n - 1, b + 1))
                if b:
                    v.wait_ge(sem(st + "_xT"), st.at("_xT", b))
                layernorm(v, st, "_in", lambda t: x_tok[:, TPB * b + t, :], b).then_inc(sem(st + "_in_norm"), 1)
                v.wait_ge(sem(st + "_xh"), st.at("_xh", b + 1))
                nc.vector.tensor_tensor(xl[:, b, :], TR[:, :], xh[:, b, :].bitcast(F32), ALU.subtract).then_inc(
                    sem(st + "_xl"), 1)
                v.wait_ge(sem(st + "_logits"), st.at("_logits", b + 1))
                lg = MISC[:, 0:TPB * E].rearrange("p (t e) -> p t e", e=E)
                if m.gated:
                    link(nc.vector.tensor_tensor(logits[:, :, :], lg, gate_bias[:, :].unsqueeze(1).broadcast_to([P, TPB, E]),
                                                 ALU.add))
                else:
                    link(nc.vector.tensor_copy(logits[:, :, :], lg))
                for t in range(TPB):
                    ins = nc.vector.max(top[:, t, :], logits[:, t, :])
                link(ins)
                nc.vector.tensor_tensor(gap[:, :], top[:, :, 0], top[:, :, 1], ALU.subtract).then_inc(
                    sem(st + "_gap"), 1)
                for t in range(TPB):
                    ins = nc.vector.max_index(top_at[:, t, :], top[:, t, :], logits[:, t, :])
                link(ins)
                link(nc.vector.tensor_copy(top_atf[:, :, :], top_at[:, :, 0:2]))
                wide = [P, E, TPB]
                experts = iota8[:, :].unsqueeze(2).broadcast_to(wide)
                nc.vector.tensor_tensor(pick1[:, :, :], experts, top_atf[:, :, 0].unsqueeze(1).broadcast_to(wide),
                                        ALU.is_equal)
                nc.vector.tensor_tensor(pick2[:, :, :], experts, top_atf[:, :, 1].unsqueeze(1).broadcast_to(wide),
                                        ALU.is_equal)
                v.wait_ge(sem(st + "_tanh"), st.at("_tanh", b + 1))
                s = 0.5 * m.combine_scale
                nc.vector.tensor_scalar(w_first[:, :], tanh_gap[:, :], s, s, ALU.mult, ALU.add)
                link(nc.vector.tensor_scalar(w_second[:, :], tanh_gap[:, :], -s, s, ALU.mult, ALU.add))
                nc.vector.tensor_tensor(pick1[:, :, :], pick1[:, :, :],
                                        w_first[:, :].unsqueeze(1).broadcast_to(wide), ALU.mult)
                link(nc.vector.tensor_tensor(pick2[:, :, :], pick2[:, :, :],
                                             w_second[:, :].unsqueeze(1).broadcast_to(wide), ALU.mult))
                nc.vector.tensor_tensor(comb[:, :, :], pick1[:, :, :], pick2[:, :, :], ALU.add).then_inc(
                    sem(st + "_comb"), 1)
                if not m.gated:
                    v.wait_ge(sem(st + "_shared_act"), st.at("_shared_act", b + 1))
                    nc.vector.tensor_scalar_mul(acc[:, b, :], acc[:, b, :], 0.5).then_inc(sem(st + "_acc_init"), 1)

            def first(e, par, c16):
                if not m.gated:
                    return
                k = 16 * e + c16
                c = c16 % HC
                v.wait_ge(sem(st + "_act"), st.at("_act", k + 1))
                if later(k - 3):
                    v.wait_ge(sem(st + "_lo"), st.at("_lo", k - 3))
                nc.vector.scalar_tensor_tensor(
                    hid[:, c16 % 4, :], UP_LIN[c16 % 2][:, :], raw[:, par, m.bias_lin + c:m.bias_lin + c + 1],
                    act_ring[:, c16 % 2, :], ALU.add, ALU.mult).then_inc(sem(st + "_hid"), 1)

            def second(e, c16):
                k = 16 * e + c16
                if not m.gated:
                    v.wait_ge(sem(st + "_act"), st.at("_act", k + 1))
                    if later(k - 3):
                        v.wait_ge(sem(st + "_down"), st.at("_down", k - 3))
                    nc.vector.tensor_copy(hid_h[:, c16 % 4, :], hid[:, c16 % 4, :]).then_inc(sem(st + "_hi"), 1)
                v.wait_ge(sem(st + "_hi"), st.at("_hi", k + 1))
                nc.vector.tensor_tensor(hid_l[:, c16 % 4, :], hid[:, c16 % 4, :], hid_h[:, c16 % 4, :].bitcast(F32),
                                        ALU.subtract).then_inc(sem(st + "_lo"), 1)

            def scale(e, par, b, i=None):
                u = NBLK * e + b
                v.wait_ge(sem(st + "_down"), st.at("_down", HC * (u + 1)))
                if b == 0:
                    turn = 16 * (e // 2 + 1) if isinstance(e, int) else i
                    v.wait_ge(sem(st + f"_comb_in{par}"), st.at(f"_comb_in{par}", turn))
                if later(u - 1):
                    v.wait_ge(sem(st + "_acc"), st.at("_acc", u - 1))
                nc.vector.scalar_tensor_tensor(scaled[:, b % 2, :], DOWN[b % 2][:, :], raw[:, par, m.bias_out:m.bias_out + 1],
                                               comb_bc[:, par, b, :], ALU.add, ALU.mult).then_inc(
                    sem(st + "_scaled"), 1)

            def expert(e, par, last, turn=None, prev_turn=None):
                for c16 in range(16):
                    if c16 < 15:
                        first(e, par, c16 + 1)
                    elif not last:
                        first(e + 1, 1 - par, 0)
                    second(e, c16)
                    if c16 % HC == 1:
                        b = c16 // HC
                        if b:
                            scale(e, par, b - 1, turn)
                        elif not (isinstance(e, int) and e == 0):
                            scale(e - 1, 1 - par, NBLK - 1)
                if last:
                    scale(e, par, NBLK - 1)

            first(0, 0, 0)
            expert(0, 0, False)
            with v.Fori(0, E // 2 - 1) as i:
                expert(2 * i + 1, 1, False, 16 * i + 16)
                expert(2 * i + 2, 0, False, 16 * i + 32)
            expert(E - 1, 1, True)
            for b in range(NBLK):
                v.wait_ge(sem(st + "_outT"), st.at("_outT", b + 1))
                xb = x_tok[:, TPB * b:TPB * (b + 1), :]
                trb = TR[:, :].rearrange("p (t d) -> p t d", d=D)
                if m.gated:
                    ins = nc.vector.tensor_tensor(xb, xb, trb, ALU.add)
                    ins.then_inc(x_done(n), 1)
                    v.wait_ge(x_done(n), x_at(n, b + 1))
                    nc.vector.sem_inc(sem(st + "_outT_read"), 1)
                else:
                    link(layernorm(v, st, "_out", lambda t: TR[:, t * P:(t + 1) * P], b))
                    nc.vector.sem_inc(sem(st + "_outT_read"), 1)
                    wide = [P, TPB, D]
                    link(nc.vector.tensor_tensor(xn_tok[:, :, :], xn_tok[:, :, :],
                                                 half_gamma[:, :].unsqueeze(1).broadcast_to(wide), ALU.mult))
                    link(nc.vector.tensor_tensor(xb, xb, half_beta[:, :].unsqueeze(1).broadcast_to(wide), ALU.add))
                    nc.vector.tensor_tensor(xb, xb, xn_tok[:, :, :], ALU.add).then_inc(x_done(n), 1)

        G = 2 * QC

        def attn_sp(sp, n, st, m):
            if n:
                sp.wait_ge(x_done(n - 1), x_at(n - 1, NBLK))
            sp.dma_start(attn_raw[:, :], attn_pack).then_inc(sem(st + "_raw_in"), 16)

        def attn_pool(pool, n, st, m):
            if n:
                pool.wait_ge(x_done(n - 1), x_at(n - 1, NBLK))
            zero = [xa_h[:, :, 0:PAD].bitcast(F32), xa_l[:, :, 0:PAD].bitcast(F32),
                    k_sb[HD:2 * HD, :, :, :, 0, :], k_sb[0:HD, :, :, :, 1, :]]
            for k, x in enumerate(zero):
                pool.memset(x, 0.0).then_inc(sem(st + "_pad"), 1)
                pool.wait_ge(sem(st + "_pad"), st.at("_pad", k + 1))
            with pool.Fori(0, NBLK) as i:
                pool.wait_ge(sem(st + "_in_var"), st.at("_in_var", i + 1))
                pool.tensor_tensor(rstd[:, :], var_eps[:, :], neghalf[:, :], ALU.pow).then_inc(sem(st + "_in_rstd"), 1)
                pool.wait_ge(sem(st + "_xl"), st.at("_xl", i + 1))
                for w, x in ((win_h, xa_h), (win_l, xa_l)):
                    for s in range(2):
                        for at, src in ((0, x[:, s, 0:T].rearrange("p (q k) -> p q k", k=QW)),
                                        (QW, x[:, s, PAD:PAD + T].rearrange("p (q k) -> p q k", k=QW)),
                                        (2 * QW, x[:, s, PAD:PAD + SINK].unsqueeze(1).broadcast_to([P, QC, SINK]))):
                            k = src.shape[2]
                            ins = pool.tensor_tensor(w[:, s, :, at:at + k], src.bitcast(F32),
                                                     one[:, :].unsqueeze(2).broadcast_to([P, QC, k]), ALU.mult)
                            ins.then_inc(sem(st + "_win"), 1)
                for g in range(G):
                    pool.wait_ge(sem(st + "_rowinv"), st.at("_rowinv", G * i + g + 1))
                    pr = probs[:, g % 4, :, :]
                    pool.tensor_tensor(pr, pr, rowinv[:, g % 4, :].unsqueeze(2).broadcast_to([P, KVH, KEYS]),
                                       ALU.mult).then_inc(sem(st + "_probs"), 1)

        def attn_act(act, n, st, m):
            with act.Fori(0, NBLK) as i:
                act.wait_ge(sem(st + "_xT"), st.at("_xT", i + 1))
                act.activation(xa_h[:, :, PAD:PAD + T], TR[:, :].rearrange("p (s t) -> p s t", s=2),
                               ACT.Copy).then_inc(sem(st + "_xh"), 1)
                for j in range(8):
                    act.wait_ge(sem(st + "_qk"), st.at("_qk", 16 * i + j + 1))
                    act.activation(q_sb[:, :, j // 4, j % 4, :],
                                   banks[j % 2][:, :].rearrange("p (g w) -> p g w", w=QW),
                                   ACT.Copy).then_inc(sem(st + "_qk_read"), 1)
                for j in range(8):
                    s, p2, h = j // 4, j // 2 % 2, j % 2
                    w = QC * KEYS // 2
                    act.wait_ge(sem(st + "_qk"), st.at("_qk", 16 * i + 8 + j + 1))
                    q = slice(h * QC // 2, (h + 1) * QC // 2)
                    for half in range(2):
                        rows = slice(HD * half, HD * half + HD)
                        ins = act.activation(k_sb[rows, s, p2, q, half, :],
                                             banks[j % 2][rows, 0:w].rearrange("p (q k) -> p q k", k=KEYS), ACT.Copy)
                    ins.then_inc(sem(st + "_qk_read"), 1)
                for g in range(G + 3):
                    if g < G:
                        act.wait_ge(sem(st + "_centred"), st.at("_centred", G * i + g + 1))
                        act.activation(probs[:, g % 4, :, :], scores[:, g % 2, :, :], ACT.Exp).then_inc(
                            sem(st + "_exp"), 1)
                    if 2 <= g < G + 2:
                        h = g - 2
                        act.wait_ge(sem(st + "_probsT"), st.at("_probsT", G * i + h + 1))
                        act.activation(probsT[:, h % 2, :], banks[4 + h % 2][0:KEYS, :], ACT.Copy).then_inc(
                            sem(st + "_probsT_read"), 1)
                    if g >= 3:
                        h = g - 3
                        act.wait_ge(sem(st + "_y"), st.at("_y", G * i + h + 1))
                        act.activation(yh[:, :, h * QW:(h + 1) * QW],
                                       banks[6 + h % 2][:, 0:8 * QW].rearrange("p (j w) -> p j w", w=QW),
                                       ACT.Copy).then_inc(sem(st + "_yh"), 1)

        def attn_pe(pe, n, st, m):
            if n:
                pe.wait_ge(x_done(n - 1), x_at(n - 1, NBLK))
            with pe.Fori(0, NBLK) as i:
                pe.wait_ge(sem(st + "_in_norm"), st.at("_in_norm", i + 1))
                for t in range(TPB):
                    ins = nc.tensor.transpose(TR[:, t * P:(t + 1) * P], xn_tok[:, t, :], ident[:, :])
                ins.then_inc(sem(st + "_xT"), 1)
                pe.wait_ge(sem(st + "_pad"), st.at("_pad", 4))
                pe.wait_ge(sem(st + "_w_lo"), st.at("_w_lo", 5))
                pe.wait_ge(sem(st + "_xl"), st.at("_xl", i + 1))
                for j in range(8):
                    if j >= 2:
                        pe.wait_ge(sem(st + "_qk_read"), st.at("_qk_read", 16 * i + j - 1))
                    c = slice(QCOL + j * P, QCOL + (j + 1) * P)
                    three(pe, banks[j % 2][:, :], ah[:, c], al[:, c], xa_h[:, :, PAD:PAD + T],
                          xa_l[:, :, PAD:PAD + T]).then_inc(sem(st + "_qk"), 1)
                pe.wait_ge(sem(st + "_win"), st.at("_win", 12 * i + 12))
                for j in range(8):
                    s, p2, h = j // 4, j // 2 % 2, j % 2
                    pe.wait_ge(sem(st + "_qk_read"), st.at("_qk_read", 16 * i + 8 + j - 1))
                    c = slice(KCOL + p2 * P, KCOL + (p2 + 1) * P)
                    q = slice(h * QC // 2, (h + 1) * QC // 2)
                    three(pe, banks[j % 2][:, 0:QC * KEYS // 2], ah[:, c], al[:, c], win_h[:, s, q, :],
                          win_l[:, s, q, :]).then_inc(sem(st + "_qk"), 1)
                pe.wait_ge(sem(st + "_qk_read"), st.at("_qk_read", 16 * i + 16))
                c = slice(VCOL, VCOL + KVH * HD)
                for j in range(8):
                    if j >= 2:
                        pe.wait_ge(sem(st + "_v_read"), st.at("_v_read", 8 * i + j - 1))
                    for h in range(2):
                        g = 2 * j + h
                        s, q = g // QC, g % QC
                        ins = three(pe, banks[j % 2][0:KEYS, h * 256:(h + 1) * 256], win_h[:, s, q, :],
                                    win_l[:, s, q, :], ah[:, c], al[:, c])
                    ins.then_inc(sem(st + "_v"), 1)

                def score(g):
                    s, q = g // QC, g % QC
                    if g >= 2:
                        pe.wait_ge(sem(st + "_masked"), st.at("_masked", G * i + g - 1))
                    for p2 in range(2):
                        ins = nc.tensor.matmul(banks[2 + g % 2][:, p2 * 2 * KEYS:(p2 + 1) * 2 * KEYS],
                                               q_sb[:, g, p2, :, :].rearrange("p r w -> p (r w)"),
                                               k_sb[:, s, p2, q, :, :].rearrange("p h k -> p (h k)"),
                                               start=True, stop=True)
                    ins.then_inc(sem(st + "_scores"), 1)

                def turn(g):
                    pe.wait_ge(sem(st + "_probs"), st.at("_probs", G * i + g + 1))
                    if g >= 2:
                        pe.wait_ge(sem(st + "_probsT_read"), st.at("_probsT_read", G * i + g - 1))
                    for kv in range(KVH):
                        ins = nc.tensor.transpose(banks[4 + g % 2][0:KEYS, kv * P:(kv + 1) * P], probs[:, g % 4, kv, :],
                                                  ident[:, :])
                    ins.then_inc(sem(st + "_probsT"), 1)

                def mix(g):
                    pe.wait_ge(sem(st + "_probsT_read"), st.at("_probsT_read", G * i + g + 1))
                    if g == 0:
                        pe.wait_ge(sem(st + "_v_read"), st.at("_v_read", 8 * i + 8))
                    if g >= 2:
                        pe.wait_ge(sem(st + "_yl"), st.at("_yl", G * i + g - 1))
                    for kv in range(KVH):
                        half, p2 = kv % 2, kv // 2
                        ins = nc.tensor.matmul(banks[6 + g % 2][HD * half:HD * half + HD, p2 * P:(p2 + 1) * P],
                                               v_sb[:, g, kv * HD:(kv + 1) * HD], probsT[:, g % 2, kv * P:(kv + 1) * P],
                                               start=True, stop=True)
                    ins.then_inc(sem(st + "_y"), 1)

                for g in range(G + 4):
                    if g < G:
                        score(g)
                    if 3 <= g < G + 3:
                        turn(g - 3)
                    if g >= 4:
                        mix(g - 4)
                pe.wait_ge(sem(st + "_yl"), st.at("_yl", G * i + G))
                for t in range(TPB):
                    for j in range(8):
                        c = slice(OCOL + j * P, OCOL + (j + 1) * P)
                        tok = slice(t * P, (t + 1) * P)
                        ins = three(pe, banks[0][:, t * P:(t + 1) * P], yh[:, j, tok], yl[:, j, tok], ah[:, c], al[:, c],
                                    start=j == 0, stop=j == 7)
                ins.then_inc(sem(st + "_wo"), 1)

        def attn_dve(v, n, st, m):
            if n:
                v.wait_ge(x_done(n - 1), x_at(n - 1, NBLK))
            v.wait_ge(sem(st + "_raw_in"), st.at("_raw_in", 16))
            for c in range(5):
                cols = slice(c * 512, (c + 1) * 512)
                nc.vector.tensor_copy(ah[:, cols], attn_raw[:, cols]).then_inc(sem(st + "_w_hi"), 1)
                v.wait_ge(sem(st + "_w_hi"), st.at("_w_hi", c + 1))
                nc.vector.tensor_tensor(al[:, cols], attn_raw[:, cols], ah[:, cols].bitcast(F32),
                                        ALU.subtract).then_inc(sem(st + "_w_lo"), 1)
            with v.Fori(0, NBLK) as i:
                if n == 0:
                    v.wait_ge(x_done(-1), x_at(-1, NBLK))

                def tile(t):
                    return x_tok[:, bass.ds(TPB * i + t, 1), :].rearrange("p a d -> p (a d)")

                for t in range(TPB):
                    nc.vector.bn_stats(stats[:, t, :], tile(t)).then_inc(sem(st + "_in_stats"), 1)
                v.wait_ge(sem(st + "_in_stats"), st.at("_in_stats", TPB * i + TPB))
                nc.vector.memset(var_eps[:, :], EPS)
                for t in range(TPB):
                    nc.vector.bn_aggr(meanvar[:, t, :], stats[:, t, :]).then_inc(sem(st + "_in_mean"), 1)
                v.wait_ge(sem(st + "_in_mean"), st.at("_in_mean", TPB * i + TPB))
                nc.vector.tensor_scalar_add(var_eps[:, :], meanvar[:, :, 1], EPS).then_inc(sem(st + "_in_var"), 1)
                v.wait_ge(sem(st + "_in_rstd"), st.at("_in_rstd", i + 1))
                for t in range(TPB):
                    ins = nc.vector.tensor_scalar(xn_tok[:, t, :], tile(t), meanvar[:, t, 0:1], rstd[:, t:t + 1],
                                                  ALU.subtract, ALU.mult)
                ins.then_inc(sem(st + "_in_norm"), 1)
                v.wait_ge(sem(st + "_xh"), st.at("_xh", i + 1))
                nc.vector.tensor_tensor(xa_l[:, :, PAD:PAD + T], TR[:, :].rearrange("p (s t) -> p s t", s=2),
                                        xa_h[:, :, PAD:PAD + T].bitcast(F32), ALU.subtract).then_inc(sem(st + "_xl"), 1)
                for j in range(8):
                    v.wait_ge(sem(st + "_v"), st.at("_v", 8 * i + j + 1))
                    nc.vector.tensor_copy(v_sb[:, 2 * j:2 * j + 2, :],
                                          banks[j % 2][0:KEYS, :].rearrange("p (g c) -> p g c", g=2)).then_inc(
                        sem(st + "_v_read"), 1)
                wide = [P, KVH, KEYS]
                for g in range(G + 4):
                    if g < G:
                        q = min(g % QC, 2)
                        sc = scores[:, g % 2, :, :]
                        v.wait_ge(sem(st + "_scores"), st.at("_scores", G * i + g + 1))
                        nc.vector.scalar_tensor_tensor(
                            sc, banks[2 + g % 2][:, 0:KVH * KEYS].rearrange("p (h k) -> p h k", k=KEYS), HD ** -0.5,
                            mask[:, q, :].unsqueeze(1).broadcast_to(wide), ALU.mult, ALU.add).then_inc(
                            sem(st + "_masked"), 1)
                        v.wait_ge(sem(st + "_masked"), st.at("_masked", G * i + g + 1))
                        nc.vector.tensor_reduce(rowmax[:, :], sc, AX.X, ALU.max).then_inc(sem(st + "_rowmax"), 1)
                        v.wait_ge(sem(st + "_rowmax"), st.at("_rowmax", G * i + g + 1))
                        nc.vector.tensor_tensor(sc, sc, rowmax[:, :].unsqueeze(2).broadcast_to(wide),
                                                ALU.subtract).then_inc(sem(st + "_centred"), 1)
                    if 1 <= g < G + 1:
                        h = g - 1
                        v.wait_ge(sem(st + "_exp"), st.at("_exp", G * i + h + 1))
                        nc.vector.tensor_reduce(rowsum[:, h % 4, :], probs[:, h % 4, :, :], AX.X, ALU.add).then_inc(
                            sem(st + "_rowsum"), 1)
                        v.wait_ge(sem(st + "_rowsum"), st.at("_rowsum", 2 * G * i + 2 * h + 1))
                        nc.vector.tensor_scalar_max(rowsum[:, h % 4, :], rowsum[:, h % 4, :], TINY).then_inc(
                            sem(st + "_rowsum"), 1)
                        v.wait_ge(sem(st + "_rowsum"), st.at("_rowsum", 2 * G * i + 2 * h + 2))
                        nc.vector.reciprocal(rowinv[:, h % 4, :], rowsum[:, h % 4, :]).then_inc(sem(st + "_rowinv"), 1)
                    if g >= 4:
                        h = g - 4
                        v.wait_ge(sem(st + "_yh"), st.at("_yh", G * i + h + 1))
                        nc.vector.tensor_tensor(yl[:, :, h * QW:(h + 1) * QW],
                                                banks[6 + h % 2][:, 0:8 * QW].rearrange("p (j w) -> p j w", w=QW),
                                                yh[:, :, h * QW:(h + 1) * QW].bitcast(F32), ALU.subtract).then_inc(
                            sem(st + "_yl"), 1)
                v.wait_ge(sem(st + "_wo"), st.at("_wo", i + 1))
                xb = x_tok[:, bass.ds(TPB * i, TPB), :]
                nc.vector.tensor_tensor(xb, xb, banks[0][:, :].rearrange("p (t d) -> p t d", d=D),
                                        ALU.add).then_inc(x_done(n), 1)

        def rwkv_sp(sp, n, st, m):
            if n:
                sp.wait_ge(x_done(n - 1), x_at(n - 1, NBLK))
            sp.dma_start(mix_raw[:, :], rwkv_pack).then_inc(sem(st + "_raw_in"), 16)
            sp.dma_start(mix_cols[:, :], rwkv_cols).then_inc(sem(st + "_raw_in"), 16)

        def rwkv_pool(pool, n, st, m):
            if n:
                pool.wait_ge(x_done(n - 1), x_at(n - 1, NBLK))
            zero = [(xs_h[:, :, 0:1].bitcast(F32), 0.0), (xs_l[:, :, 0:1].bitcast(F32), 0.0), (mm[:, :, 0:1], NEG_INF),
                    (pp[:, :, 0:1], NEG_INF), (aa[:, :, 0:1], 0.0)]
            for k, (x, value) in enumerate(zero):
                pool.memset(x, value).then_inc(sem(st + "_pad"), 1)
                pool.wait_ge(sem(st + "_pad"), st.at("_pad", k + 1))
            for b in range(NBLK):
                rstd_pool(pool, st, "_in", b)
                rstd_pool(pool, st, "_ln1", b)
            for b in range(NBLK):
                rstd_pool(pool, st, "_ln2", b)
                pool.wait_ge(sem(st + "_x1"), st.at("_x1", b + 1))
                xb, x1 = x_tok[:, TPB * b:TPB * (b + 1), :], xin[:, TPB * b:TPB * (b + 1), :]
                pool.tensor_tensor(xb, xb, x1, ALU.add).then_inc(sem(st + "_x_x1"), 1)

        def seqs(b):
            return slice(2 * b, 2 * b + 2)

        def two(ap):
            return ap.rearrange("p (s t) -> p s t", s=2)

        def rwkv_act(act, n, st, m):
            act.wait_ge(sem(st + "_raw_in"), st.at("_raw_in", 32))

            def affine_hi(bank, g, name, count):
                act.wait_ge(sem(st + name + "T"), st.at(name + "T", count + 1))
                if count:
                    act.wait_ge(sem(st + name + "_lo"), st.at(name + "_lo", count))
                act.activation(xf[:, :, :], two(bank[:, :]), ACT.Identity, scale=mix_cols[:, g:g + 1],
                               bias=mix_cols[:, g + 1:g + 2]).then_inc(sem(st + name + "_f"), 1)
                act.wait_ge(sem(st + name + "_f"), st.at(name + "_f", count + 1))
                act.activation(xs_h[:, seqs(count), 1:T + 1], xf[:, :, :], ACT.Copy).then_inc(
                    sem(st + name + "_hi"), 1)

            for b in range(NBLK):
                affine_hi(TR, C_G1, "_xa", b)
                for j, (dst, f) in enumerate(((kf, ACT.Copy), (vf, ACT.Copy), (sr, ACT.Sigmoid))):
                    act.wait_ge(sem(st + "_kvr"), st.at("_kvr", 3 * b + j + 1))
                    act.activation(dst[:, seqs(b), :], two(banks[j][:, :]), f).then_inc(sem(st + "_kvr_read"), 1)
            for b in range(NBLK):
                for r in range(2):
                    act.wait_ge(sem(st + "_clip"), st.at("_clip", 2 * b + r + 1))
                    act.activation(t1[:, :, :], t1[:, :, :], ACT.Exp, scale=-1.0)
                    act.activation(t2[:, :, :], t2[:, :, :], ACT.Exp).then_inc(sem(st + "_decay"), 1)
                    if r == 0:
                        act.wait_ge(sem(st + "_ss"), st.at("_ss", b + 1))
                        act.activation(ss[:, :, :], ss[:, :, :], ACT.Ln).then_inc(sem(st + "_ln_ss"), 1)
            for b in range(NBLK):
                act.wait_ge(sem(st + "_va"), st.at("_va", b + 1))
                if b:
                    act.wait_ge(sem(st + "_z"), st.at("_z", b))
                act.activation(q_mix[:, :, :], gap_kp[:, seqs(b), :], ACT.Sigmoid,
                               bias=mix_cols[:, C_U:C_U + 1]).then_inc(sem(st + "_q"), 1)

            def head(b):
                affine_hi(banks[7], C_G2, "_xb", b)

            def body(b):
                act.wait_ge(sem(st + "_cr"), st.at("_cr", b + 1))
                if b:
                    act.wait_ge(sem(st + "_out_c"), st.at("_out_c", b))
                act.activation(sig_c[:, :], banks[2][:, :], ACT.Sigmoid).then_inc(sem(st + "_sig_c"), 1)
                for c in range(HC):
                    k = HC * b + c
                    act.wait_ge(sem(st + "_ck"), st.at("_ck", k + 1))
                    if later(k - 1):
                        act.wait_ge(sem(st + "_kc"), st.at("_kc", k - 1))
                    act.activation(relu[:, k % 2, :], banks[k % 2][:, :], ACT.Relu).then_inc(sem(st + "_relu"), 1)
                    act.wait_ge(sem(st + "_kc"), st.at("_kc", k + 1))
                    if later(k - 1):
                        act.wait_ge(sem(st + "_cv"), st.at("_cv", k - 1))
                    act.activation(kc_h[:, k % 2, :], kc[:, k % 2, :], ACT.Copy).then_inc(sem(st + "_kc_hi"), 1)

            head(0)
            for b in range(NBLK):
                if b + 1 < NBLK:
                    head(b + 1)
                body(b)

        def rwkv_pe(pe, n, st, m):
            def shifted(dst, cols, b):
                three(pe, dst, mix_h[:, 0, cols], mix_l[:, 0, cols], xs_h[:, seqs(b), 1:T + 1],
                      xs_l[:, seqs(b), 1:T + 1], stop=False)
                return three(pe, dst, mix_h[:, 1, cols], mix_l[:, 1, cols], xs_h[:, seqs(b), 0:T],
                             xs_l[:, seqs(b), 0:T], start=False)

            def transposes(dst, src):
                for t in range(TPB):
                    ins = nc.tensor.transpose(dst[:, t * P:(t + 1) * P], src(t), ident[:, :])
                return ins

            if n:
                pe.wait_ge(x_done(n - 1), x_at(n - 1, NBLK))
            pe.wait_ge(sem(st + "_pad"), st.at("_pad", 5))
            for b in range(NBLK):
                pe.wait_ge(sem(st + "_ln1_norm"), st.at("_ln1_norm", b + 1))
                if b:
                    pe.wait_ge(sem(st + "_xa_f"), st.at("_xa_f", b))
                transposes(TR, lambda t: xn_tok[:, t, :]).then_inc(sem(st + "_xaT"), 1)
                pe.wait_ge(sem(st + "_xa_lo"), st.at("_xa_lo", b + 1))
                if b == 0:
                    pe.wait_ge(sem(st + "_w_ready"), st.at("_w_ready", 1))
                for j, c in enumerate((KW, VW, RW)):
                    if later(3 * (b - 1) + j + 1):
                        pe.wait_ge(sem(st + "_kvr_read"), st.at("_kvr_read", 3 * (b - 1) + j + 1))
                    shifted(banks[j][:, :], slice(c, c + P), b).then_inc(sem(st + "_kvr"), 1)

            def head(b):
                pe.wait_ge(sem(st + "_z"), st.at("_z", b + 1))
                if b == 0:
                    pe.wait_ge(sem(st + "_xa_f"), st.at("_xa_f", NBLK))
                else:
                    pe.wait_ge(sem(st + "_x1"), st.at("_x1", b))
                if b >= 2:
                    pe.wait_ge(x_done(n), x_at(n, b - 1))
                transposes(TR, lambda t: zf[:, 2 * b + t // 2, t % 2 * P:(t % 2 + 1) * P]).then_inc(sem(st + "_zT"), 1)
                pe.wait_ge(sem(st + "_ln2_norm"), st.at("_ln2_norm", b + 1))
                if b:
                    pe.wait_ge(sem(st + "_xb_f"), st.at("_xb_f", b))
                transposes(banks[7], lambda t: xn_tok[:, t, :]).then_inc(sem(st + "_xbT"), 1)

            def body(b):
                pe.wait_ge(sem(st + "_xb_lo"), st.at("_xb_lo", b + 1))
                if b == 0:
                    pe.wait_ge(sem(st + "_kvr_read"), st.at("_kvr_read", 3 * NBLK))
                else:
                    pe.wait_ge(sem(st + "_sig_c"), st.at("_sig_c", b))
                shifted(banks[2][:, :], slice(CRW, CRW + P), b).then_inc(sem(st + "_cr"), 1)

                def up(c):
                    k = HC * b + c
                    if later(k - 1):
                        pe.wait_ge(sem(st + "_relu"), st.at("_relu", k - 1))
                    shifted(banks[k % 2][:, :], slice(CKW + c * P, CKW + (c + 1) * P), b).then_inc(sem(st + "_ck"), 1)

                def down(c):
                    k = HC * b + c
                    pe.wait_ge(sem(st + "_kc_lo"), st.at("_kc_lo", k + 1))
                    if c == 0:
                        if later(b - 1):
                            pe.wait_ge(sem(st + "_out_c"), st.at("_out_c", b - 1))
                    three(pe, banks[4 + b % 2][:, :], cv_h[:, c * P:(c + 1) * P], cv_l[:, c * P:(c + 1) * P],
                          kc_h[:, k % 2, :], kc_l[:, k % 2, :], start=c == 0, stop=c == HC - 1).then_inc(
                        sem(st + "_cv"), 1)

                up(0)
                up(1)
                for c in range(HC):
                    down(c)
                    if c + 2 < HC:
                        up(c + 2)
                pe.wait_ge(sem(st + "_out_c"), st.at("_out_c", b + 1))
                pe.wait_ge(sem(st + "_x1"), st.at("_x1", min(b + 2, NBLK)))
                transposes(TR, lambda t: out_c[:, t * P:(t + 1) * P]).then_inc(sem(st + "_outT"), 1)

            head(0)
            for b in range(NBLK):
                if b + 1 < NBLK:
                    if b:
                        pe.wait_ge(x_done(n), x_at(n, b))
                    head(b + 1)
                body(b)

        def rwkv_dve(v, n, st, m):
            v.wait_ge(sem(st + "_raw_in"), st.at("_raw_in", 32))
            if n:
                v.wait_ge(x_done(n - 1), x_at(n - 1, NBLK))
            link(nc.vector.tensor_scalar(one_minus[:, :], mix_cols[:, C_RK:C_RK + 5], -1.0, 1.0, ALU.mult, ALU.add))
            places = ((KW, VW), (VW, RW), (RW, CKW), (CKW, CRW), (CRW, CVW))
            for side in range(2):
                for j, (lo, hi) in enumerate(places):
                    scale = mix_cols[:, C_RK + j:C_RK + j + 1] if side == 0 else one_minus[:, j:j + 1]
                    ins = nc.vector.tensor_scalar_mul(mix_f[:, lo:hi], mix_raw[:, lo:hi], scale)
                link(ins)
                link(nc.vector.tensor_copy(mix_h[:, side, :], mix_f[:, :]))
                link(nc.vector.tensor_tensor(mix_l[:, side, :], mix_f[:, :], mix_h[:, side, :].bitcast(F32),
                                             ALU.subtract))
            link(nc.vector.tensor_copy(cv_h[:, :], mix_raw[:, CVW:RWKV_COLS]))
            nc.vector.tensor_tensor(cv_l[:, :], mix_raw[:, CVW:RWKV_COLS], cv_h[:, :].bitcast(F32),
                                    ALU.subtract).then_inc(sem(st + "_w_ready"), 1)

            def rest(name, b):
                v.wait_ge(sem(st + name + "_hi"), st.at(name + "_hi", b + 1))
                nc.vector.tensor_tensor(xs_l[:, seqs(b), 1:T + 1], xf[:, :, :], xs_h[:, seqs(b), 1:T + 1].bitcast(F32),
                                        ALU.subtract).then_inc(sem(st + name + "_lo"), 1)

            for b in range(NBLK):
                if n == 0:
                    v.wait_ge(x_done(-1), x_at(-1, NBLK))
                link(layernorm(v, st, "_in", lambda t: x_tok[:, TPB * b + t, :], b,
                               lambda t: xin[:, TPB * b + t, :]))
                if b:
                    v.wait_ge(sem(st + "_xaT"), st.at("_xaT", b))
                layernorm(v, st, "_ln1", lambda t: xin[:, TPB * b + t, :], b).then_inc(sem(st + "_ln1_norm"), 1)
                rest("_xa", b)
            v.wait_ge(sem(st + "_pad"), st.at("_pad", 5))
            for b in range(NBLK):
                k, vv, gp = kf[:, seqs(b), :], vf[:, seqs(b), :], gap_kp[:, seqs(b), :]
                w = mix_cols[:, C_W:C_W + 1].broadcast_to([P, T])
                v.wait_ge(sem(st + "_kvr_read"), st.at("_kvr_read", 3 * b + 3))
                for s in range(2):
                    ins = nc.vector.tensor_tensor_scan(mm[:, s, 1:T + 1], kf[:, 2 * b + s, :], w, NEG_INF, ALU.max,
                                                       ALU.add)
                link(ins)

                def clips(gap):
                    nc.vector.tensor_scalar_max(t1[:, :, :], gap, 0.0)
                    nc.vector.tensor_scalar_min(t2[:, :, :], gap, 0.0).then_inc(sem(st + "_clip"), 1)

                link(nc.vector.tensor_tensor(gp, k, mm[:, :, 0:T], ALU.subtract))
                clips(gp)
                v.wait_ge(sem(st + "_decay"), st.at("_decay", 2 * b + 1))
                for s in range(2):
                    ins = nc.vector.tensor_tensor_scan(ss[:, s, :], t1[:, s, :], t2[:, s, :], 1.0, ALU.mult, ALU.add)
                ins.then_inc(sem(st + "_ss"), 1)
                v.wait_ge(sem(st + "_ln_ss"), st.at("_ln_ss", b + 1))
                link(nc.vector.tensor_tensor(pp[:, :, 1:T + 1], mm[:, :, 1:T + 1], ss[:, :, :], ALU.add))
                link(nc.vector.tensor_tensor(gp, k, pp[:, :, 0:T], ALU.subtract))
                clips(gp)
                v.wait_ge(sem(st + "_decay"), st.at("_decay", 2 * b + 2))
                link(nc.vector.tensor_tensor(t2[:, :, :], t2[:, :, :], vv, ALU.mult))
                for s in range(2):
                    ins = nc.vector.tensor_tensor_scan(aa[:, s, 1:T + 1], t1[:, s, :], t2[:, s, :], 0.0, ALU.mult,
                                                       ALU.add)
                link(ins)
                nc.vector.tensor_copy(y_mix[:, seqs(b), :], aa[:, :, 0:T])
                nc.vector.tensor_tensor(vv, vv, aa[:, :, 0:T], ALU.subtract).then_inc(sem(st + "_va"), 1)
            for b in range(NBLK):
                y, z = y_mix[:, seqs(b), :], zf[:, seqs(b), :]
                v.wait_ge(sem(st + "_q"), st.at("_q", b + 1))
                link(nc.vector.tensor_tensor(z, q_mix[:, :, :], vf[:, seqs(b), :], ALU.mult))
                link(nc.vector.tensor_tensor(z, z, y, ALU.add))
                nc.vector.tensor_tensor(z, z, sr[:, seqs(b), :], ALU.mult).then_inc(sem(st + "_z"), 1)

            def head(b):
                v.wait_ge(sem(st + "_zT"), st.at("_zT", b + 1))
                x1 = xin[:, TPB * b:TPB * (b + 1), :]
                nc.vector.tensor_tensor(x1, x1, TR[:, :].rearrange("p (t d) -> p t d", d=D), ALU.add).then_inc(
                    sem(st + "_x1"), 1)
                v.wait_ge(sem(st + "_x1"), st.at("_x1", b + 1))
                if b == 0:
                    v.wait_ge(sem(st + "_xaT"), st.at("_xaT", NBLK))
                else:
                    v.wait_ge(sem(st + "_xbT"), st.at("_xbT", b))
                layernorm(v, st, "_ln2", lambda t: xin[:, TPB * b + t, :], b).then_inc(sem(st + "_ln2_norm"), 1)
                rest("_xb", b)

            def body(b):
                for c in range(HC):
                    k = HC * b + c
                    v.wait_ge(sem(st + "_relu"), st.at("_relu", k + 1))
                    if later(k - 1):
                        v.wait_ge(sem(st + "_kc_lo"), st.at("_kc_lo", k - 1))
                    nc.vector.tensor_tensor(kc[:, k % 2, :], relu[:, k % 2, :], relu[:, k % 2, :], ALU.mult).then_inc(
                        sem(st + "_kc"), 1)
                    v.wait_ge(sem(st + "_kc_hi"), st.at("_kc_hi", k + 1))
                    nc.vector.tensor_tensor(kc_l[:, k % 2, :], kc[:, k % 2, :], kc_h[:, k % 2, :].bitcast(F32),
                                            ALU.subtract).then_inc(sem(st + "_kc_lo"), 1)
                v.wait_ge(sem(st + "_cv"), st.at("_cv", HC * (b + 1)))
                v.wait_ge(sem(st + "_sig_c"), st.at("_sig_c", b + 1))
                if b:
                    v.wait_ge(sem(st + "_outT"), st.at("_outT", b))
                nc.vector.tensor_tensor(out_c[:, :], banks[4 + b % 2][:, :], sig_c[:, :], ALU.mult).then_inc(
                    sem(st + "_out_c"), 1)
                v.wait_ge(sem(st + "_outT"), st.at("_outT", b + 1))
                v.wait_ge(sem(st + "_x_x1"), st.at("_x_x1", b + 1))
                xb = x_tok[:, TPB * b:TPB * (b + 1), :]
                nc.vector.tensor_tensor(xb, xb, TR[:, :].rearrange("p (t d) -> p t d", d=D), ALU.add).then_inc(
                    x_done(n), 1)

            head(0)
            for b in range(NBLK):
                if b + 1 < NBLK:
                    head(b + 1)
                body(b)

        GLU, MLP = Moe("glu", True), Moe("mlp", False)
        parts = {"rwkv": (None, rwkv_sp, rwkv_pool, rwkv_act, rwkv_pe, rwkv_dve),
                 "attn": (None, attn_sp, attn_pool, attn_act, attn_pe, attn_dve),
                 "glu": (GLU, moe_sp, moe_pool, moe_act, moe_pe, moe_dve),
                 "mlp": (MLP, moe_sp, moe_pool, moe_act, moe_pe, moe_dve)}

        @block.sync
        def _(sp):
            for b in range(NBLK):
                sp.dma_start(x_tok[:, TPB * b:TPB * (b + 1), :],
                             x_in.rearrange("b (t p) d -> p (b t) d", p=P)[:, TPB * b:TPB * (b + 1), :]).then_inc(
                    sem("x_loaded"), 16)
            sp.dma_start(gate_raw["glu"][:, :], glu_gate).then_inc(sem("small_in"), 16)
            sp.dma_start(gate_raw["mlp"][:, :], mlp_gate).then_inc(sem("small_in"), 16)
            sp.dma_start(shared_raw[:, :], mlp_shared).then_inc(sem("small_in"), 16)
            sp.dma_start(gate_bias[:, :], glu_gate_b.broadcast_to([P, E])).then_inc(sem("small_in"), 16)
            sp.dma_start(half_gamma[:, :], mlp_rows[0:1, :].broadcast_to([P, D])).then_inc(sem("small_in"), 16)
            sp.dma_start(half_beta[:, :], mlp_rows[1:2, :].broadcast_to([P, D])).then_inc(sem("small_in"), 16)
            for n, (st, kind) in enumerate(order):
                parts[kind][1](sp, n, st, parts[kind][0])
            for b in range(NBLK):
                sp.wait_ge(x_done(len(order) - 1), x_at(len(order) - 1, b + 1))
                sp.dma_start(out.rearrange("b (t p) d -> p (b t) d", p=P)[:, TPB * b:TPB * (b + 1), :],
                             x_tok[:, TPB * b:TPB * (b + 1), :]).then_inc(sem("stored"), 16)
            sp.wait_ge(sem("stored"), 16 * NBLK)

        @block.gpsimd
        def _(pool):
            pool.memset(ident[:, :], 0.0).then_inc(sem("ident_zero"), 1)
            pool.memset(one[:, :], 1.0)
            pool.memset(neghalf[:, :], -0.5).then_inc(sem("neghalf_set"), 1)
            pool.wait_ge(sem("ident_zero"), 1)
            pool.affine_select(out=ident[:, :], in_=ident[:, :], compare_op=ALU.not_equal, fill=1.0, base=0,
                               pattern=[[-1, P]], channel_multiplier=1).then_inc(sem("ident_set"), 1)
            pool.wait_ge(sem("neghalf_set"), 1)
            steps = [0]

            def then(ins):
                steps[0] += 1
                ins.then_inc(sem("mask_step"), 1)
                pool.wait_ge(sem("mask_step"), steps[0])

            then(pool.memset(mask[:, :, :], 0.0))
            for r in range(4):
                rows = mask[r * QW:(r + 1) * QW, :, 0:2 * QW]
                then(pool.affine_select(out=rows, in_=rows, compare_op=ALU.is_ge, fill=MASKED, base=QW,
                                        pattern=[[0, 3], [-1, 2 * QW]], channel_multiplier=1))
                then(pool.affine_select(out=rows, in_=rows, compare_op=ALU.is_ge, fill=MASKED, base=-1,
                                        pattern=[[0, 3], [1, 2 * QW]], channel_multiplier=-1))
                rows = mask[r * QW:(r + 1) * QW, 0, 2 * QW:KEYS]
                then(pool.affine_select(out=rows, in_=rows, compare_op=ALU.is_ge, fill=MASKED, base=0,
                                        pattern=[[-1, SINK]], channel_multiplier=1))
            then(pool.memset(mask[:, 0, 0:QW + SINK], MASKED))
            then(pool.memset(mask[:, 1, 0:SINK], MASKED))
            for n, (st, kind) in enumerate(order):
                parts[kind][2](pool, n, st, parts[kind][0])

        @block.scalar
        def _(act):
            for n, (st, kind) in enumerate(order):
                parts[kind][3](act, n, st, parts[kind][0])

        @block.tensor
        def _(pe):
            pe.wait_ge(sem("ident_set"), 1)
            for n, (st, kind) in enumerate(order):
                parts[kind][4](pe, n, st, parts[kind][0])

        @block.vector
        def _(v):
            for e in range(E):
                ins = nc.vector.memset(iota8[:, e:e + 1], float(e))
            link(ins)
            v.wait_ge(sem("small_in"), 16 * 6)
            v.wait_ge(sem("mask_step"), 15)
            nc.vector.tensor_scalar_mul(half_gamma[:, :], half_gamma[:, :], 0.5)
            nc.vector.tensor_scalar_mul(half_beta[:, :], half_beta[:, :], 0.5)
            for g in ("glu", "mlp"):
                link(nc.vector.tensor_copy(gate_h[g][:, :], gate_raw[g][:, :]))
                nc.vector.tensor_tensor(gate_l[g][:, :], gate_raw[g][:, :], gate_h[g][:, :].bitcast(F32), ALU.subtract)
            link(nc.vector.tensor_copy(shared_h[:, :], shared_raw[:, 0:D]))
            nc.vector.tensor_tensor(shared_l[:, :], shared_raw[:, 0:D], shared_h[:, :].bitcast(F32),
                                    ALU.subtract).then_inc(sem("const_ready"), 1)
            for n, (st, kind) in enumerate(order):
                parts[kind][5](v, n, st, parts[kind][0])


def _layout(i):
    import numpy as np

    def a(name):
        return np.ascontiguousarray(np.asarray(i[name]))

    def col(v):
        return v.reshape(-1, 128).T

    def pack(ups, down, biases):
        per = []
        for e in range(E):
            down_e = down[e].reshape(HC, 128, 128).transpose(1, 0, 2).reshape(128, 512)
            per.append(np.concatenate([u[e] for u in ups] + [down_e] + [col(b[e]) for b in biases], axis=1))
        return np.ascontiguousarray(np.concatenate(per, axis=1))

    glu = pack([a("L0_ffn_W0"), a("L0_ffn_W1")], a("L0_ffn_W2"), [a("L0_ffn_b0"), a("L0_ffn_b1"), a("L0_ffn_b2")])
    mlp = pack([a("L1_ffn_W1")], a("L1_ffn_W2"), [a("L1_ffn_b1"), a("L1_ffn_b2")])
    shared = np.concatenate([a("L1_ffn_shared_W"), col(a("L1_ffn_shared_b"))], axis=1)
    wq = a("L0_attn_Wq").reshape(D, 2, 2, 4, HD).transpose(0, 1, 3, 2, 4).reshape(D, 1024)
    wo = a("L0_attn_Wo").reshape(2, 2, 4, HD, D).transpose(1, 3, 0, 2, 4).reshape(D, 1024)
    attn = np.concatenate([wq, a("L0_attn_Wk"), a("L0_attn_Wv"), wo], axis=1)
    cv = a("L1_attn_Wcv").T.reshape(HC, 128, 128).transpose(1, 0, 2).reshape(128, 512)
    rwkv = np.concatenate([a("L1_attn_Wk").T, a("L1_attn_Wv").T, a("L1_attn_Wr").T, a("L1_attn_Wck").T,
                           a("L1_attn_Wcr").T, cv], axis=1)
    cols = np.stack([a("L1_attn_" + n) for n in ("w", "u", "rk", "rv", "rr", "crk", "crr", "ln1_g", "ln1_b", "ln2_g",
                                                 "ln2_b")], axis=1)
    rows = np.stack([a("L1_ffn_gamma"), a("L1_ffn_beta")])
    return {
        "x_in": a("L0_attn_X"), "glu_pack": glu, "glu_gate": a("L0_ffn_Wg"), "glu_gate_b": a("L0_ffn_bg")[None, :],
        "mlp_pack": mlp, "mlp_gate": a("L1_ffn_gate_W"), "mlp_shared": shared, "mlp_rows": rows,
        "attn_pack": attn, "rwkv_pack": rwkv, "rwkv_cols": cols,
    }


def kernel(**inputs):
    import concourse.bacc as bacc
    from concourse.bass_utils import run_bass_kernel_spmd

    nc = bacc.Bacc("TRN2", target_bir_lowering=False, num_devices=1)
    arrays = _layout(inputs)
    args = [nc.dram_tensor(n, x.shape, mybir.dt.from_np(x.dtype), kind="ExternalInput").ap()
            for n, x in arrays.items()]
    args.append(nc.dram_tensor("out", (B, T, D), F32, kind="ExternalOutput").ap())
    build_program(nc, *args)
    return run_bass_kernel_spmd(nc, [arrays], core_ids=[0]).results[0]["out"]
```

```python
import concourse.bass as bass
from concourse import mybir
from contextlib import ExitStack

F32 = mybir.dt.float32
R32 = mybir.dt.float32r
U32 = mybir.dt.uint32
ALU = mybir.AluOpType
ACT = mybir.ActivationFunctionType
AX = mybir.AxisListType

P = 128
B, T, D = 8, 256, 128
NT = B * T // P
NBLK = 4
TPB = NT // NBLK
BC = TPB * P
E = 8
HC = 4
EPS = 1e-5
AHEAD = 3

GLU_COLS = 3 * 512 + 2 * HC + 1
MLP_COLS = 2 * 512 + HC + 1

HD, KVH = 64, 4
QW, SINK = 32, 4
QC = T // QW
KEYS = 2 * QW + SINK
PAD = QW
ATTN_COLS = 1024 + 256 + 256 + 1024
QCOL, KCOL, VCOL, OCOL = 0, 1024, 1280, 1536
MASKED = -3.0e38
TINY = 1.1754943508222875e-38


KW, VW, RW, CKW, CRW, CVW, RWKV_COLS = 0, 128, 256, 384, 896, 1024, 1536
C_W, C_U, C_RK, C_RV, C_RR, C_CRK, C_CRR, C_G1, C_B1, C_G2, C_B2, N_COLS = range(12)
NEG_INF = -1e38


class Moe:

    def __init__(self, name, gated):
        self.name, self.gated = name, gated
        self.ups = 2 if gated else 1
        self.cols = GLU_COLS if gated else MLP_COLS
        self.wcols = (self.ups + 1) * 512
        self.bias_lin = self.wcols
        self.bias_act = self.wcols + HC * (self.ups - 1)
        self.bias_out = self.bias_act + HC
        self.combine_scale = 0.5 if gated else 1.0
        self.func = ACT.Silu if gated else ACT.Gelu


def signals_of_one_use(kind, what):
    chunks, units = E * NBLK * HC, E * NBLK
    pieces = 3 if kind == "glu" else 2
    return {"_up": chunks, "_act": chunks, "_hid": chunks, "_hi": chunks, "_lo": chunks, "_down": chunks,
            "_scaled": units, "_acc": units, "_wh": pieces * E, "_w_ready": pieces * E,
            "_raw_in0": 16 * E // 2, "_raw_in1": 16 * E // 2, "_comb_in0": 16 * E // 2, "_comb_in1": 16 * E // 2,
            "_comb_out": 16, "_logits": NBLK, "_gap": 1, "_tanh": 1,
            "_comb": 1, "_combT": 1, "_comb_rows": 1, "_acc_init": 1 if kind == "glu" else NBLK}.get(what, NBLK)


class Stage:

    def __init__(self, kind, use):
        self.kind, self.use = kind, use

    def __add__(self, what):
        return self.kind + what

    def at(self, what, value):
        return value + self.use * signals_of_one_use(self.kind, what) if self.use else value


def later(value):
    return not isinstance(value, int) or value > 0


def build_program(nc, x_in, glu_pack, glu_gate, glu_gate_b, mlp_pack, mlp_gate, mlp_shared, mlp_rows,
                  attn_pack, rwkv_pack, rwkv_cols, out, stages=("glu", "attn", "glu", "mlp", "rwkv", "mlp")):
    ctx = ExitStack()
    with ctx:
        def sb(name, shape, dt=F32):
            return ctx.enter_context(nc.sbuf_tensor(name, shape, dt))

        sems = {}

        def sem(name):
            if name not in sems:
                sems[name] = ctx.enter_context(nc.semaphore(name))
            return sems[name]

        x_tok = sb("x_tok", [P, NT, D])
        ident = sb("ident", [P, P])
        iota8 = sb("iota8", [P, E])
        one = sb("one", [P, 1])
        neghalf = sb("neghalf", [P, TPB])
        stats = sb("stats", [P, 2, TPB, 6])
        meanvar = sb("meanvar", [P, 2, TPB, 2])
        var_eps = sb("var_eps", [P, 2, TPB])
        rstd = sb("rstd", [P, 2, TPB])
        xn_tok = sb("xn_tok", [P, 2, TPB, D])
        comb_dram = nc.dram_tensor("comb_scratch", [E, NT * P], F32)

        banks = [ctx.enter_context(nc.psum_tensor(f"bank{i}", [P, 512], F32)) for i in range(8)]
        UP_ACT, UP_LIN, DOWN = banks[0:2], banks[2:4], banks[4:6]
        TRS = banks[6:8]
        TR = TRS[0]

        raw = sb("raw_weights", [P, 2, GLU_COLS])
        wh = sb("weights_hi", [P, 2, 1536], R32)
        wl = sb("weights_lo", [P, 2, 1536], R32)
        gate_raw = {"glu": sb("glu_gate_raw", [P, E]), "mlp": sb("mlp_gate_raw", [P, E])}
        gate_h = {n: sb(n + "_gate_hi", [P, E], R32) for n in ("glu", "mlp")}
        gate_l = {n: sb(n + "_gate_lo", [P, E], R32) for n in ("glu", "mlp")}
        gate_bias = sb("gate_bias", [P, E])
        shared_raw = sb("shared_raw", [P, D + 1])
        shared_h = sb("shared_hi", [P, D], R32)
        shared_l = sb("shared_lo", [P, D], R32)
        half_gamma = sb("half_gamma", [P, D])
        half_beta = sb("half_beta", [P, D])
        logits = sb("logits", [P, NT, E])
        top = sb("top", [P, NT, 8])
        top_at = sb("top_at", [P, NT, 8], U32)
        top_atf = sb("top_atf", [P, NT, 2])
        gap = sb("gap", [P, NT])
        tanh_gap = sb("tanh_gap", [P, NT])
        w_first = sb("w_first", [P, NT])
        w_second = sb("w_second", [P, NT])
        pick1 = sb("pick1", [P, E, NT])
        pick2 = sb("pick2", [P, E, NT])
        comb = sb("comb", [P, E, NT])
        comb_rows = sb("comb_rows", [E * NT, P])
        acc = sb("acc", [P, NBLK, BC])
        mask = sb("mask", [P, 3, KEYS])

        def shared_place(*tensors):
            with ExitStack() as place:
                return [place.enter_context(nc.sbuf_tensor(n, s, d)) for n, s, d in tensors]

        xh, xl, comb_bc, act_ring, hid, hid_h, hid_l, scaled = shared_place(
            ("xh", [P, NBLK, BC], R32), ("xl", [P, NBLK, BC], R32),
            ("comb_bc", [P, 2, NBLK, BC], F32), ("act_ring", [P, 2, BC], F32), ("hid", [P, 4, BC], F32),
            ("hid_hi", [P, 4, BC], R32), ("hid_lo", [P, 4, BC], R32), ("scaled", [P, 2, BC], F32))
        (attn_raw, ah, al, xa_h, xa_l, win_h, win_l, q_sb, k_sb, v_sb, yh, yl, scores, probs, probsT, rowmax, rowsum,
         rowinv) = shared_place(
            ("attn_raw", [P, ATTN_COLS], F32), ("attn_hi", [P, ATTN_COLS], R32), ("attn_lo", [P, ATTN_COLS], R32),
            ("xa_hi", [P, 2, PAD + T], R32), ("xa_lo", [P, 2, PAD + T], R32),
            ("win_hi", [P, 2, QC, KEYS], R32), ("win_lo", [P, 2, QC, KEYS], R32),
            ("q_sb", [P, 2 * QC, 2, 4, QW], F32), ("k_sb", [P, 2, 2, QC, 2, KEYS], F32),
            ("v_sb", [KEYS, 2 * QC, KVH * HD], F32), ("y_hi", [P, 8, BC], R32), ("y_lo", [P, 8, BC], R32),
            ("scores", [P, 2, KVH, KEYS], F32), ("probs", [P, 4, KVH, KEYS], F32), ("probsT", [KEYS, 2, KVH * P], F32),
            ("rowmax", [P, KVH], F32), ("rowsum", [P, 4, KVH], F32), ("rowinv", [P, 4, KVH], F32))

        (mix_raw, mix_cols, one_minus, mix_f, mix_h, mix_l, cv_h, cv_l, xs_h, xs_l, xin, xf, kf, vf, sr, mm, pp, aa,
         t1, t2, ss, gap_kp, q_mix, zf, relu, kc, kc_h, kc_l, sig_c, out_c) = shared_place(
            ("mix_raw", [P, RWKV_COLS], F32), ("mix_cols", [P, N_COLS], F32), ("one_minus", [P, 5], F32),
            ("mix_f", [P, 1024], F32), ("mix_hi", [P, 2, 1024], R32), ("mix_lo", [P, 2, 1024], R32),
            ("cv_hi", [P, 512], R32), ("cv_lo", [P, 512], R32),
            ("xs_hi", [P, B, T + 1], R32), ("xs_lo", [P, B, T + 1], R32), ("xin", [P, NT, D], F32),
            ("xf", [P, 2, T], F32), ("kf", [P, B, T], F32), ("vf", [P, B, T], F32), ("sr", [P, B, T], F32),
            ("mm", [P, 2, T + 1], F32), ("pp", [P, 2, T + 1], F32), ("aa", [P, 2, T + 1], F32),
            ("t1", [P, 2, T], F32), ("t2", [P, 2, T], F32), ("ss", [P, 2, T], F32), ("gap_kp", [P, B, T], F32),
            ("q_mix", [P, 2, T], F32), ("zf", [P, B, T], F32), ("relu", [P, 2, BC], F32), ("kc", [P, 2, BC], F32),
            ("kc_hi", [P, 2, BC], R32), ("kc_lo", [P, 2, BC], R32), ("sig_c", [P, BC], F32), ("out_c", [P, BC], F32))
        y_mix = kf

        order = [(Stage(kind, stages[:n].count(kind)), kind) for n, kind in enumerate(stages)]

        def x_done(n):
            return sem("x_loaded") if n < 0 else sem(order[n][0] + "_x_done")

        def x_at(n, blocks):
            return 16 * NBLK if n < 0 else order[n][0].at("_x_done", blocks)

        chain = [0]

        def link(ins):
            chain[0] += 1
            ins.then_inc(sem("dve_chain"), 1)
            nc.vector.wait_ge(sem("dve_chain"), chain[0])

        block = ctx.enter_context(nc.Block())

        def moe_load(sp, n, st, m, e, par):
            pack = glu_pack if m.gated else mlp_pack
            if later(4 * (e - 1)):
                sp.wait_ge(sem(st + "_scaled"), st.at("_scaled", 4 * (e - 1)))
            sp.dma_start(raw[:, par, 0:m.cols], pack[:, bass.ds(e * m.cols, m.cols)]).then_inc(
                sem(st + f"_raw_in{par}"), 16)

        def moe_load_comb(sp, n, st, m, e, par):
            src = comb_dram.ap()[bass.ds(e, 1), :].rearrange("e (b n) -> e b n", b=NBLK).broadcast_to([P, NBLK, BC])
            sp.dma_start(comb_bc[:, par, :, :], src).then_inc(sem(st + f"_comb_in{par}"), 16)

        def moe_sp(sp, n, st, m):
            old = [order[i][0] for i in range(n) if stages[i] in ("glu", "mlp")]
            if old:
                sp.wait_ge(sem(old[-1] + "_scaled"), old[-1].at("_scaled", NBLK * E))
            moe_load(sp, n, st, m, 0, 0)
            moe_load(sp, n, st, m, 1, 1)
            sp.wait_ge(sem(st + "_comb_rows"), st.at("_comb_rows", 1))
            sp.dma_start(comb_dram.ap().rearrange("e (t p) -> (e t) p", p=P), comb_rows[:, :]).then_inc(
                sem(st + "_comb_out"), 16)
            sp.wait_ge(sem(st + "_comb_out"), st.at("_comb_out", 16))
            moe_load_comb(sp, n, st, m, 0, 0)
            moe_load_comb(sp, n, st, m, 1, 1)
            with sp.Fori(0, E // 2 - 1) as i:
                for par in range(2):
                    sp.wait_ge(sem(st + "_scaled"), st.at("_scaled", 8 * i + 4 * (par + 1)))
                    sp.dma_start(raw[:, par, 0:m.cols],
                                 (glu_pack if m.gated else mlp_pack)[:, bass.ds((2 * i + par + 2) * m.cols, m.cols)]
                                 ).then_inc(sem(st + f"_raw_in{par}"), 16)
                    moe_load_comb(sp, n, st, m, 2 * i + par + 2, par)

        def moe_split_piece(pool, st, m, count, slot, piece):
            cols = slice(piece * 512, piece * 512 + 512)
            pool.tensor_tensor(wh[:, slot, cols], raw[:, slot, cols], one[:, :].broadcast_to([P, 512]),
                               ALU.mult).then_inc(sem(st + "_wh"), 1)
            pool.wait_ge(sem(st + "_wh"), st.at("_wh", count + 1))
            pool.tensor_tensor(wl[:, slot, cols], raw[:, slot, cols], wh[:, slot, cols].bitcast(F32),
                               ALU.subtract).then_inc(sem(st + "_w_ready"), 1)

        def rstd_pool(pool, st, name, n, slot=0):
            pool.wait_ge(sem(st + name + "_var"), st.at(name + "_var", n + 1))
            pool.tensor_tensor(rstd[:, slot, :], var_eps[:, slot, :], neghalf[:, :], ALU.pow).then_inc(
                sem(st + name + "_rstd"), 1)

        def moe_pool(pool, n, st, m):
            pieces = m.ups + 1
            pool.wait_ge(sem(st + "_raw_in0"), st.at("_raw_in0", 16))
            old = [order[i][0] for i in range(n) if stages[i] in ("glu", "mlp")]
            if old:
                pool.wait_ge(sem(old[-1] + "_down"), old[-1].at("_down", HC * NBLK * E))
            for c in range(pieces):
                moe_split_piece(pool, st, m, c, 0, c)
                rstd_pool(pool, st, "_in", c, c % 2)
            for b in range(pieces, NBLK):
                rstd_pool(pool, st, "_in", b, b % 2)
            if m.gated:
                pool.memset(acc[:, :, :], 0.0).then_inc(sem(st + "_acc_init"), 1)
                pool.wait_ge(sem(st + "_acc_init"), st.at("_acc_init", 1))
            else:
                pool.wait_ge(sem(st + "_acc_init"), st.at("_acc_init", NBLK))

            def expert(e, par, last, next_load=None):
                for b in range(NBLK):
                    u = NBLK * e + b
                    pool.wait_ge(sem(st + "_scaled"), st.at("_scaled", u + 1))
                    if later(u):
                        pool.wait_ge(sem(st + "_acc"), st.at("_acc", u))
                    pool.tensor_tensor(acc[:, b, :], acc[:, b, :], scaled[:, b % 2, :],
                                       ALU.add).then_inc(sem(st + "_acc"), 1)
                    if last:
                        if not m.gated and b in (1, 2):
                            rstd_pool(pool, st, "_out", b - 1, (b - 1) % 2)
                        continue
                    if b == 0:
                        pool.wait_ge(sem(st + f"_raw_in{1 - par}"), st.at(f"_raw_in{1 - par}", next_load))
                    for piece in ((0, 1), (2,), (), ())[b][:pieces]:
                        if piece < pieces:
                            moe_split_piece(pool, st, m, pieces * (e + 1) + piece, 1 - par, piece)

            expert(0, 0, False, 16)
            with pool.Fori(0, E // 2 - 1) as i:
                expert(2 * i + 1, 1, False, 16 * i + 32)
                expert(2 * i + 2, 0, False, 16 * i + 32)
            expert(E - 1, 1, True)
            if not m.gated:
                for b in (2, 3):
                    rstd_pool(pool, st, "_out", b, b % 2)

        def moe_act(act, n, st, m):
            def enter(b):
                act.wait_ge(sem(st + "_xT"), st.at("_xT", b + 1))
                act.activation(xh[:, b, :], TRS[b % 2][:, :], ACT.Copy).then_inc(sem(st + "_xh"), 1)

            def shared(b):
                if not m.gated:
                    act.wait_ge(sem(st + "_shared"), st.at("_shared", b + 1))
                    act.activation(acc[:, b, :], UP_LIN[b % 2][:, :], ACT.Gelu,
                                   bias=shared_raw[:, D:D + 1]).then_inc(sem(st + "_shared_act"), 1)

            enter(0)
            for b in range(NBLK):
                if b + 1 < NBLK:
                    enter(b + 1)
                shared(b)
            act.wait_ge(sem(st + "_gap"), st.at("_gap", 1))
            act.activation(tanh_gap[:, :], gap[:, :], ACT.Tanh, scale=0.5).then_inc(sem(st + "_tanh"), 1)
            act.wait_ge(sem(st + "_combT"), st.at("_combT", 1))
            act.activation(comb_rows[:, :], TRS[1][:, 0:P], ACT.Copy).then_inc(sem(st + "_comb_rows"), 1)

            def first(e, par, c16):
                k = 16 * e + c16
                c = c16 % HC
                act.wait_ge(sem(st + "_up"), st.at("_up", k + 1))
                dst = act_ring[:, k16(c16) % 2, :] if m.gated else hid[:, c16 % 4, :]
                if not m.gated:
                    if later(k - 3):
                        act.wait_ge(sem(st + "_lo"), st.at("_lo", k - 3))
                act.activation(dst, UP_ACT[c16 % 2][:, :], m.func,
                               bias=raw[:, par, m.bias_act + c:m.bias_act + c + 1]).then_inc(sem(st + "_act"), 1)

            def k16(c16):
                return c16

            def second(e, c16):
                k = 16 * e + c16
                act.wait_ge(sem(st + ("_hid" if m.gated else "_act")), st.at(("_hid" if m.gated else "_act"), k + 1))
                if later(k - 3):
                    act.wait_ge(sem(st + "_down"), st.at("_down", k - 3))
                act.activation(hid_h[:, c16 % 4, :], hid[:, c16 % 4, :], ACT.Copy).then_inc(sem(st + "_hi"), 1)

            def expert(e, par, last):
                for c16 in range(16):
                    if c16 < 15:
                        first(e, par, c16 + 1)
                    elif not last:
                        first(e + 1, 1 - par, 0)
                    if m.gated:
                        second(e, c16)

            first(0, 0, 0)
            expert(0, 0, False)
            with act.Fori(0, E // 2 - 1) as i:
                expert(2 * i + 1, 1, False)
                expert(2 * i + 2, 0, False)
            expert(E - 1, 1, True)

        def three(pe, dst, w_h, w_l, v_h, v_l, start=True, stop=True):
            nc.tensor.matmul(dst, w_h, v_h, start=start, stop=False)
            nc.tensor.matmul(dst, w_h, v_l, start=False, stop=False)
            return nc.tensor.matmul(dst, w_l, v_h, start=False, stop=stop)

        def moe_pe(pe, n, st, m):
            g = "glu" if m.gated else "mlp"
            def enter(b):
                pe.wait_ge(sem(st + "_in_norm"), st.at("_in_norm", b + 1))
                if b >= 2:
                    pe.wait_ge(sem(st + "_xl"), st.at("_xl", b - 1))
                for t in range(TPB):
                    ins = nc.tensor.transpose(TRS[b % 2][:, t * P:(t + 1) * P], xn_tok[:, b % 2, t, :], ident[:, :])
                ins.then_inc(sem(st + "_xT"), 1)

            def gates(b):
                pe.wait_ge(sem(st + "_xl"), st.at("_xl", b + 1))
                if not m.gated:
                    if b >= 2:
                        pe.wait_ge(sem(st + "_shared_act"), st.at("_shared_act", b - 1))
                    three(pe, UP_LIN[b % 2][:, :], shared_h[:, :], shared_l[:, :], xh[:, b, :], xl[:, b, :]).then_inc(
                        sem(st + "_shared"), 1)
                for t in range(TPB):
                    tok = slice(t * P, (t + 1) * P)
                    at = (TPB * b + t) * E
                    ins = three(pe, DOWN[1][:, at:at + E], xh[:, b, tok], xl[:, b, tok], gate_h[g][:, :],
                                gate_l[g][:, :])
                ins.then_inc(sem(st + "_logits"), 1)

            if n:
                pe.wait_ge(x_done(n - 1), x_at(n - 1, NBLK))
            pe.wait_ge(sem("const_ready"), 1)
            enter(0)
            for b in range(NBLK):
                if b + 1 < NBLK:
                    enter(b + 1)
                gates(b)

            def spread_combine():
                pe.wait_ge(sem(st + "_comb"), st.at("_comb", 1))
                nc.tensor.transpose(TRS[1][:, 0:P], comb[:, :, :].rearrange("p e t -> p (e t)"),
                                    ident[:, :]).then_inc(sem(st + "_combT"), 1)

            def up(e, par, c16):
                k = 16 * e + c16
                b, c = c16 // HC, c16 % HC
                if c16 == 0:
                    pe.wait_ge(sem(st + "_w_ready"), st.at("_w_ready", (m.ups + 1) * (e + 1)))
                if later(k - 1):
                    pe.wait_ge(sem(st + ("_hid" if m.gated else "_act")), st.at(("_hid" if m.gated else "_act"), k - 1))
                if m.gated:
                    cols = slice(c * P, c * P + P)
                    three(pe, UP_LIN[c16 % 2][:, :], wh[:, par, cols], wl[:, par, cols], xh[:, b, :], xl[:, b, :])
                o = (m.ups - 1) * 512
                cols = slice(o + c * P, o + c * P + P)
                three(pe, UP_ACT[c16 % 2][:, :], wh[:, par, cols], wl[:, par, cols], xh[:, b, :],
                      xl[:, b, :]).then_inc(sem(st + "_up"), 1)

            def down(e, par, c16):
                k = 16 * e + c16
                b, c = c16 // HC, c16 % HC
                pe.wait_ge(sem(st + "_lo"), st.at("_lo", k + 1))
                if c == 0:
                    if later(NBLK * e + b - 1):
                        pe.wait_ge(sem(st + "_scaled"), st.at("_scaled", NBLK * e + b - 1))
                o = m.ups * 512 + c * P
                three(pe, DOWN[b % 2][:, :], wh[:, par, o:o + P], wl[:, par, o:o + P], hid_h[:, c16 % 4, :],
                      hid_l[:, c16 % 4, :], start=c == 0, stop=c == HC - 1).then_inc(sem(st + "_down"), 1)

            def leave(b):
                pe.wait_ge(sem(st + "_acc"), st.at("_acc", NBLK * (E - 1) + b + 1))
                if b >= 2:
                    pe.wait_ge(sem(st + "_outT_read"), st.at("_outT_read", b - 1))
                for t in range(TPB):
                    ins = nc.tensor.transpose(TRS[b % 2][:, t * P:(t + 1) * P], acc[:, b, t * P:(t + 1) * P],
                                              ident[:, :])
                ins.then_inc(sem(st + "_outT"), 1)

            def expert(e, par, last):
                for c16 in range(16):
                    if last and c16 in (8, 12):
                        leave((c16 - 8) // 4)
                    if c16 < 16 - AHEAD:
                        up(e, par, c16 + AHEAD)
                    elif not last:
                        up(e + 1, 1 - par, c16 - (16 - AHEAD))
                    down(e, par, c16)

            for c16 in range(AHEAD):
                up(0, 0, c16)
                if c16 == 1:
                    spread_combine()
            expert(0, 0, False)
            with pe.Fori(0, E // 2 - 1) as i:
                expert(2 * i + 1, 1, False)
                expert(2 * i + 2, 0, False)
            expert(E - 1, 1, True)
            leave(2)
            leave(3)

        def moments(v, st, name, src, slot=0):
            for t in range(TPB):
                ins = nc.vector.bn_stats(stats[:, slot, t, :], src(t))
            link(ins)
            for t in range(TPB):
                ins = nc.vector.bn_aggr(meanvar[:, slot, t, :], stats[:, slot, t, :])
            link(ins)
            nc.vector.tensor_scalar_add(var_eps[:, slot, :], meanvar[:, slot, :, 1], EPS).then_inc(
                sem(st + name + "_var"), 1)

        def normalise(v, st, name, src, n, slot=0, dst=None):
            v.wait_ge(sem(st + name + "_rstd"), st.at(name + "_rstd", n + 1))
            dst = dst or (lambda t: xn_tok[:, slot, t, :])
            for t in range(TPB):
                ins = nc.vector.tensor_scalar(dst(t), src(t), meanvar[:, slot, t, 0:1], rstd[:, slot, t:t + 1],
                                              ALU.subtract, ALU.mult)
            return ins

        def layernorm(v, st, name, src, n, dst=None):
            moments(v, st, name, src)
            return normalise(v, st, name, src, n, 0, dst)

        def moe_dve(v, n, st, m):
            def tokens(b):
                return lambda t: x_tok[:, TPB * b + t, :]

            def enter_moments(b):
                v.wait_ge(x_done(n - 1), x_at(n - 1, b + 1))
                moments(v, st, "_in", tokens(b), b % 2)

            def enter_norm(b):
                if b >= 2:
                    v.wait_ge(sem(st + "_xT"), st.at("_xT", b - 1))
                normalise(v, st, "_in", tokens(b), b, b % 2).then_inc(sem(st + "_in_norm"), 1)

            def enter_rest(b):
                v.wait_ge(sem(st + "_xh"), st.at("_xh", b + 1))
                nc.vector.tensor_tensor(xl[:, b, :], TRS[b % 2][:, :], xh[:, b, :].bitcast(F32),
                                        ALU.subtract).then_inc(sem(st + "_xl"), 1)

            enter_moments(0)
            for b in range(NBLK):
                if b + 1 < NBLK:
                    enter_moments(b + 1)
                enter_norm(b)
                if b:
                    enter_rest(b - 1)
            enter_rest(NBLK - 1)
            v.wait_ge(sem(st + "_logits"), st.at("_logits", NBLK))
            lg = DOWN[1][:, 0:NT * E].rearrange("p (t e) -> p t e", e=E)
            if m.gated:
                link(nc.vector.tensor_tensor(logits[:, :, :], lg, gate_bias[:, :].unsqueeze(1).broadcast_to([P, NT, E]),
                                             ALU.add))
            else:
                link(nc.vector.tensor_copy(logits[:, :, :], lg))
            for t in range(NT):
                ins = nc.vector.max(top[:, t, :], logits[:, t, :])
            link(ins)
            nc.vector.tensor_tensor(gap[:, :], top[:, :, 0], top[:, :, 1], ALU.subtract).then_inc(sem(st + "_gap"), 1)
            for t in range(NT):
                ins = nc.vector.max_index(top_at[:, t, :], top[:, t, :], logits[:, t, :])
            link(ins)
            link(nc.vector.tensor_copy(top_atf[:, :, :], top_at[:, :, 0:2]))
            wide = [P, E, NT]
            experts = iota8[:, :].unsqueeze(2).broadcast_to(wide)
            nc.vector.tensor_tensor(pick1[:, :, :], experts, top_atf[:, :, 0].unsqueeze(1).broadcast_to(wide),
                                    ALU.is_equal)
            nc.vector.tensor_tensor(pick2[:, :, :], experts, top_atf[:, :, 1].unsqueeze(1).broadcast_to(wide),
                                    ALU.is_equal)
            v.wait_ge(sem(st + "_tanh"), st.at("_tanh", 1))
            s = 0.5 * m.combine_scale
            nc.vector.tensor_scalar(w_first[:, :], tanh_gap[:, :], s, s, ALU.mult, ALU.add)
            link(nc.vector.tensor_scalar(w_second[:, :], tanh_gap[:, :], -s, s, ALU.mult, ALU.add))
            nc.vector.tensor_tensor(pick1[:, :, :], pick1[:, :, :],
                                    w_first[:, :].unsqueeze(1).broadcast_to(wide), ALU.mult)
            link(nc.vector.tensor_tensor(pick2[:, :, :], pick2[:, :, :],
                                         w_second[:, :].unsqueeze(1).broadcast_to(wide), ALU.mult))
            nc.vector.tensor_tensor(comb[:, :, :], pick1[:, :, :], pick2[:, :, :], ALU.add).then_inc(
                sem(st + "_comb"), 1)
            if not m.gated:
                for b in range(NBLK):
                    v.wait_ge(sem(st + "_shared_act"), st.at("_shared_act", b + 1))
                    nc.vector.tensor_scalar_mul(acc[:, b, :], acc[:, b, :], 0.5).then_inc(sem(st + "_acc_init"), 1)

            def first(e, par, c16):
                if not m.gated:
                    return
                k = 16 * e + c16
                c = c16 % HC
                v.wait_ge(sem(st + "_act"), st.at("_act", k + 1))
                if later(k - 3):
                    v.wait_ge(sem(st + "_lo"), st.at("_lo", k - 3))
                nc.vector.scalar_tensor_tensor(
                    hid[:, c16 % 4, :], UP_LIN[c16 % 2][:, :], raw[:, par, m.bias_lin + c:m.bias_lin + c + 1],
                    act_ring[:, c16 % 2, :], ALU.add, ALU.mult).then_inc(sem(st + "_hid"), 1)

            def second(e, c16):
                k = 16 * e + c16
                if not m.gated:
                    v.wait_ge(sem(st + "_act"), st.at("_act", k + 1))
                    if later(k - 3):
                        v.wait_ge(sem(st + "_down"), st.at("_down", k - 3))
                    nc.vector.tensor_copy(hid_h[:, c16 % 4, :], hid[:, c16 % 4, :]).then_inc(sem(st + "_hi"), 1)
                v.wait_ge(sem(st + "_hi"), st.at("_hi", k + 1))
                nc.vector.tensor_tensor(hid_l[:, c16 % 4, :], hid[:, c16 % 4, :], hid_h[:, c16 % 4, :].bitcast(F32),
                                        ALU.subtract).then_inc(sem(st + "_lo"), 1)

            def scale(e, par, b, i=None):
                u = NBLK * e + b
                v.wait_ge(sem(st + "_down"), st.at("_down", HC * (u + 1)))
                if b == 0:
                    turn = 16 * (e // 2 + 1) if isinstance(e, int) else i
                    v.wait_ge(sem(st + f"_comb_in{par}"), st.at(f"_comb_in{par}", turn))
                if later(u - 1):
                    v.wait_ge(sem(st + "_acc"), st.at("_acc", u - 1))
                nc.vector.scalar_tensor_tensor(scaled[:, b % 2, :], DOWN[b % 2][:, :], raw[:, par, m.bias_out:m.bias_out + 1],
                                               comb_bc[:, par, b, :], ALU.add, ALU.mult).then_inc(
                    sem(st + "_scaled"), 1)

            def leave(b):
                v.wait_ge(sem(st + "_outT"), st.at("_outT", b + 1))
                xb = x_tok[:, TPB * b:TPB * (b + 1), :]
                bank = TRS[b % 2]
                if m.gated:
                    nc.vector.tensor_tensor(xb, xb, bank[:, :].rearrange("p (t d) -> p t d", d=D),
                                            ALU.add).then_inc(x_done(n), 1)
                    v.wait_ge(x_done(n), x_at(n, b + 1))
                    nc.vector.sem_inc(sem(st + "_outT_read"), 1)
                else:
                    moments(v, st, "_out", lambda t: bank[:, t * P:(t + 1) * P], b % 2)
                    link(normalise(v, st, "_out", lambda t: bank[:, t * P:(t + 1) * P], b, b % 2))
                    nc.vector.sem_inc(sem(st + "_outT_read"), 1)
                    wide = [P, TPB, D]
                    xn = xn_tok[:, b % 2, :, :]
                    link(nc.vector.tensor_tensor(xn, xn, half_gamma[:, :].unsqueeze(1).broadcast_to(wide), ALU.mult))
                    link(nc.vector.tensor_tensor(xb, xb, half_beta[:, :].unsqueeze(1).broadcast_to(wide), ALU.add))
                    nc.vector.tensor_tensor(xb, xb, xn, ALU.add).then_inc(x_done(n), 1)

            def expert(e, par, last, turn=None):
                for c16 in range(16):
                    if c16 < 15:
                        first(e, par, c16 + 1)
                    elif not last:
                        first(e + 1, 1 - par, 0)
                    second(e, c16)
                    if c16 % HC == 1:
                        b = c16 // HC
                        if b:
                            scale(e, par, b - 1, turn)
                        elif not (isinstance(e, int) and e == 0):
                            scale(e - 1, 1 - par, NBLK - 1)
                    if last and c16 in (10, 14):
                        leave((c16 - 10) // 4)
                if last:
                    scale(e, par, NBLK - 1)

            first(0, 0, 0)
            expert(0, 0, False)
            with v.Fori(0, E // 2 - 1) as i:
                expert(2 * i + 1, 1, False, 16 * i + 16)
                expert(2 * i + 2, 0, False, 16 * i + 32)
            expert(E - 1, 1, True)
            leave(2)
            leave(3)

        G = 2 * QC

        def attn_sp(sp, n, st, m):
            if n:
                sp.wait_ge(x_done(n - 1), x_at(n - 1, NBLK))
            sp.dma_start(attn_raw[:, :], attn_pack).then_inc(sem(st + "_raw_in"), 16)

        def attn_pool(pool, n, st, m):
            if n:
                pool.wait_ge(x_done(n - 1), x_at(n - 1, NBLK))
            zero = [xa_h[:, :, 0:PAD].bitcast(F32), xa_l[:, :, 0:PAD].bitcast(F32),
                    k_sb[HD:2 * HD, :, :, :, 0, :], k_sb[0:HD, :, :, :, 1, :]]
            for k, x in enumerate(zero):
                pool.memset(x, 0.0).then_inc(sem(st + "_pad"), 1)
                pool.wait_ge(sem(st + "_pad"), st.at("_pad", k + 1))
            with pool.Fori(0, NBLK) as i:
                pool.wait_ge(sem(st + "_in_var"), st.at("_in_var", i + 1))
                pool.tensor_tensor(rstd[:, 0, :], var_eps[:, 0, :], neghalf[:, :], ALU.pow).then_inc(sem(st + "_in_rstd"), 1)
                pool.wait_ge(sem(st + "_xl"), st.at("_xl", i + 1))
                for w, x in ((win_h, xa_h), (win_l, xa_l)):
                    for s in range(2):
                        for at, src in ((0, x[:, s, 0:T].rearrange("p (q k) -> p q k", k=QW)),
                                        (QW, x[:, s, PAD:PAD + T].rearrange("p (q k) -> p q k", k=QW)),
                                        (2 * QW, x[:, s, PAD:PAD + SINK].unsqueeze(1).broadcast_to([P, QC, SINK]))):
                            k = src.shape[2]
                            ins = pool.tensor_tensor(w[:, s, :, at:at + k], src.bitcast(F32),
                                                     one[:, :].unsqueeze(2).broadcast_to([P, QC, k]), ALU.mult)
                            ins.then_inc(sem(st + "_win"), 1)
                for g in range(G):
                    pool.wait_ge(sem(st + "_rowinv"), st.at("_rowinv", G * i + g + 1))
                    pr = probs[:, g % 4, :, :]
                    pool.tensor_tensor(pr, pr, rowinv[:, g % 4, :].unsqueeze(2).broadcast_to([P, KVH, KEYS]),
                                       ALU.mult).then_inc(sem(st + "_probs"), 1)

        def attn_act(act, n, st, m):
            with act.Fori(0, NBLK) as i:
                act.wait_ge(sem(st + "_xT"), st.at("_xT", i + 1))
                act.activation(xa_h[:, :, PAD:PAD + T], TR[:, :].rearrange("p (s t) -> p s t", s=2),
                               ACT.Copy).then_inc(sem(st + "_xh"), 1)
                for j in range(8):
                    act.wait_ge(sem(st + "_qk"), st.at("_qk", 16 * i + j + 1))
                    act.activation(q_sb[:, :, j // 4, j % 4, :],
                                   banks[j % 2][:, :].rearrange("p (g w) -> p g w", w=QW),
                                   ACT.Copy).then_inc(sem(st + "_qk_read"), 1)
                for j in range(8):
                    s, p2, h = j // 4, j // 2 % 2, j % 2
                    w = QC * KEYS // 2
                    act.wait_ge(sem(st + "_qk"), st.at("_qk", 16 * i + 8 + j + 1))
                    q = slice(h * QC // 2, (h + 1) * QC // 2)
                    for half in range(2):
                        rows = slice(HD * half, HD * half + HD)
                        ins = act.activation(k_sb[rows, s, p2, q, half, :],
                                             banks[j % 2][rows, 0:w].rearrange("p (q k) -> p q k", k=KEYS), ACT.Copy)
                    ins.then_inc(sem(st + "_qk_read"), 1)
                for g in range(G + 3):
                    if g < G:
                        act.wait_ge(sem(st + "_centred"), st.at("_centred", G * i + g + 1))
                        act.activation(probs[:, g % 4, :, :], scores[:, g % 2, :, :], ACT.Exp).then_inc(
                            sem(st + "_exp"), 1)
                    if 2 <= g < G + 2:
                        h = g - 2
                        act.wait_ge(sem(st + "_probsT"), st.at("_probsT", G * i + h + 1))
                        act.activation(probsT[:, h % 2, :], banks[4 + h % 2][0:KEYS, :], ACT.Copy).then_inc(
                            sem(st + "_probsT_read"), 1)
                    if g >= 3:
                        h = g - 3
                        act.wait_ge(sem(st + "_y"), st.at("_y", G * i + h + 1))
                        act.activation(yh[:, :, h * QW:(h + 1) * QW],
                                       banks[6 + h % 2][:, 0:8 * QW].rearrange("p (j w) -> p j w", w=QW),
                                       ACT.Copy).then_inc(sem(st + "_yh"), 1)
                act.wait_ge(sem(st + "_wo_T"), st.at("_wo_T", i + 1))
                act.activation(attn_raw[:, 0:BC], banks[0][:, :], ACT.Copy).then_inc(sem(st + "_wo_T_read"), 1)

        def attn_pe(pe, n, st, m):
            if n:
                pe.wait_ge(x_done(n - 1), x_at(n - 1, NBLK))
            with pe.Fori(0, NBLK) as i:
                pe.wait_ge(sem(st + "_in_norm"), st.at("_in_norm", i + 1))
                for t in range(TPB):
                    ins = nc.tensor.transpose(TR[:, t * P:(t + 1) * P], xn_tok[:, 0, t, :], ident[:, :])
                ins.then_inc(sem(st + "_xT"), 1)
                pe.wait_ge(sem(st + "_pad"), st.at("_pad", 4))
                pe.wait_ge(sem(st + "_w_lo"), st.at("_w_lo", 5))
                pe.wait_ge(sem(st + "_xl"), st.at("_xl", i + 1))
                for j in range(8):
                    if j >= 2:
                        pe.wait_ge(sem(st + "_qk_read"), st.at("_qk_read", 16 * i + j - 1))
                    c = slice(QCOL + j * P, QCOL + (j + 1) * P)
                    three(pe, banks[j % 2][:, :], ah[:, c], al[:, c], xa_h[:, :, PAD:PAD + T],
                          xa_l[:, :, PAD:PAD + T]).then_inc(sem(st + "_qk"), 1)
                pe.wait_ge(sem(st + "_win"), st.at("_win", 12 * i + 12))
                for j in range(8):
                    s, p2, h = j // 4, j // 2 % 2, j % 2
                    pe.wait_ge(sem(st + "_qk_read"), st.at("_qk_read", 16 * i + 8 + j - 1))
                    c = slice(KCOL + p2 * P, KCOL + (p2 + 1) * P)
                    q = slice(h * QC // 2, (h + 1) * QC // 2)
                    three(pe, banks[j % 2][:, 0:QC * KEYS // 2], ah[:, c], al[:, c], win_h[:, s, q, :],
                          win_l[:, s, q, :]).then_inc(sem(st + "_qk"), 1)
                pe.wait_ge(sem(st + "_qk_read"), st.at("_qk_read", 16 * i + 16))
                c = slice(VCOL, VCOL + KVH * HD)
                for j in range(8):
                    if j >= 2:
                        pe.wait_ge(sem(st + "_v_read"), st.at("_v_read", 8 * i + j - 1))
                    for h in range(2):
                        g = 2 * j + h
                        s, q = g // QC, g % QC
                        ins = three(pe, banks[j % 2][0:KEYS, h * 256:(h + 1) * 256], win_h[:, s, q, :],
                                    win_l[:, s, q, :], ah[:, c], al[:, c])
                    ins.then_inc(sem(st + "_v"), 1)

                def score(g):
                    s, q = g // QC, g % QC
                    if g >= 2:
                        pe.wait_ge(sem(st + "_masked"), st.at("_masked", G * i + g - 1))
                    for p2 in range(2):
                        ins = nc.tensor.matmul(banks[2 + g % 2][:, p2 * 2 * KEYS:(p2 + 1) * 2 * KEYS],
                                               q_sb[:, g, p2, :, :].rearrange("p r w -> p (r w)"),
                                               k_sb[:, s, p2, q, :, :].rearrange("p h k -> p (h k)"),
                                               start=True, stop=True)
                    ins.then_inc(sem(st + "_scores"), 1)

                def turn(g):
                    pe.wait_ge(sem(st + "_probs"), st.at("_probs", G * i + g + 1))
                    if g >= 2:
                        pe.wait_ge(sem(st + "_probsT_read"), st.at("_probsT_read", G * i + g - 1))
                    for kv in range(KVH):
                        ins = nc.tensor.transpose(banks[4 + g % 2][0:KEYS, kv * P:(kv + 1) * P], probs[:, g % 4, kv, :],
                                                  ident[:, :])
                    ins.then_inc(sem(st + "_probsT"), 1)

                def mix(g):
                    pe.wait_ge(sem(st + "_probsT_read"), st.at("_probsT_read", G * i + g + 1))
                    if g == 0:
                        pe.wait_ge(sem(st + "_v_read"), st.at("_v_read", 8 * i + 8))
                    if g >= 2:
                        pe.wait_ge(sem(st + "_yl"), st.at("_yl", G * i + g - 1))
                    for kv in range(KVH):
                        half, p2 = kv % 2, kv // 2
                        ins = nc.tensor.matmul(banks[6 + g % 2][HD * half:HD * half + HD, p2 * P:(p2 + 1) * P],
                                               v_sb[:, g, kv * HD:(kv + 1) * HD], probsT[:, g % 2, kv * P:(kv + 1) * P],
                                               start=True, stop=True)
                    ins.then_inc(sem(st + "_y"), 1)

                for g in range(G + 4):
                    if g < G:
                        score(g)
                    if 3 <= g < G + 3:
                        turn(g - 3)
                    if g >= 4:
                        mix(g - 4)
                pe.wait_ge(sem(st + "_yl"), st.at("_yl", G * i + G))
                for j in range(8):
                    c = slice(OCOL + j * P, OCOL + (j + 1) * P)
                    ins = three(pe, banks[0][:, :], ah[:, c], al[:, c], yh[:, j, :], yl[:, j, :],
                                start=j == 0, stop=j == 7)
                ins.then_inc(sem(st + "_wo_T"), 1)
                pe.wait_ge(sem(st + "_wo_T_read"), st.at("_wo_T_read", i + 1))
                for t in range(TPB):
                    ins = nc.tensor.transpose(banks[1][:, t * P:(t + 1) * P], attn_raw[:, t * P:(t + 1) * P],
                                              ident[:, :])
                ins.then_inc(sem(st + "_wo"), 1)

        def attn_dve(v, n, st, m):
            if n:
                v.wait_ge(x_done(n - 1), x_at(n - 1, NBLK))
            v.wait_ge(sem(st + "_raw_in"), st.at("_raw_in", 16))
            for c in range(5):
                cols = slice(c * 512, (c + 1) * 512)
                nc.vector.tensor_copy(ah[:, cols], attn_raw[:, cols]).then_inc(sem(st + "_w_hi"), 1)
                v.wait_ge(sem(st + "_w_hi"), st.at("_w_hi", c + 1))
                nc.vector.tensor_tensor(al[:, cols], attn_raw[:, cols], ah[:, cols].bitcast(F32),
                                        ALU.subtract).then_inc(sem(st + "_w_lo"), 1)
            with v.Fori(0, NBLK) as i:
                if n == 0:
                    v.wait_ge(x_done(-1), x_at(-1, NBLK))

                def tile(t):
                    return x_tok[:, bass.ds(TPB * i + t, 1), :].rearrange("p a d -> p (a d)")

                for t in range(TPB):
                    nc.vector.bn_stats(stats[:, 0, t, :], tile(t)).then_inc(sem(st + "_in_stats"), 1)
                v.wait_ge(sem(st + "_in_stats"), st.at("_in_stats", TPB * i + TPB))
                nc.vector.memset(var_eps[:, 0, :], EPS)
                for t in range(TPB):
                    nc.vector.bn_aggr(meanvar[:, 0, t, :], stats[:, 0, t, :]).then_inc(sem(st + "_in_mean"), 1)
                v.wait_ge(sem(st + "_in_mean"), st.at("_in_mean", TPB * i + TPB))
                nc.vector.tensor_scalar_add(var_eps[:, 0, :], meanvar[:, 0, :, 1], EPS).then_inc(sem(st + "_in_var"), 1)
                v.wait_ge(sem(st + "_in_rstd"), st.at("_in_rstd", i + 1))
                for t in range(TPB):
                    ins = nc.vector.tensor_scalar(xn_tok[:, 0, t, :], tile(t), meanvar[:, 0, t, 0:1], rstd[:, 0, t:t + 1],
                                                  ALU.subtract, ALU.mult)
                ins.then_inc(sem(st + "_in_norm"), 1)
                v.wait_ge(sem(st + "_xh"), st.at("_xh", i + 1))
                nc.vector.tensor_tensor(xa_l[:, :, PAD:PAD + T], TR[:, :].rearrange("p (s t) -> p s t", s=2),
                                        xa_h[:, :, PAD:PAD + T].bitcast(F32), ALU.subtract).then_inc(sem(st + "_xl"), 1)
                for j in range(8):
                    v.wait_ge(sem(st + "_v"), st.at("_v", 8 * i + j + 1))
                    nc.vector.tensor_copy(v_sb[:, 2 * j:2 * j + 2, :],
                                          banks[j % 2][0:KEYS, :].rearrange("p (g c) -> p g c", g=2)).then_inc(
                        sem(st + "_v_read"), 1)
                wide = [P, KVH, KEYS]
                for g in range(G + 4):
                    if g < G:
                        q = min(g % QC, 2)
                        sc = scores[:, g % 2, :, :]
                        v.wait_ge(sem(st + "_scores"), st.at("_scores", G * i + g + 1))
                        nc.vector.scalar_tensor_tensor(
                            sc, banks[2 + g % 2][:, 0:KVH * KEYS].rearrange("p (h k) -> p h k", k=KEYS), HD ** -0.5,
                            mask[:, q, :].unsqueeze(1).broadcast_to(wide), ALU.mult, ALU.add).then_inc(
                            sem(st + "_masked"), 1)
                        v.wait_ge(sem(st + "_masked"), st.at("_masked", G * i + g + 1))
                        nc.vector.tensor_reduce(rowmax[:, :], sc, AX.X, ALU.max).then_inc(sem(st + "_rowmax"), 1)
                        v.wait_ge(sem(st + "_rowmax"), st.at("_rowmax", G * i + g + 1))
                        nc.vector.tensor_tensor(sc, sc, rowmax[:, :].unsqueeze(2).broadcast_to(wide),
                                                ALU.subtract).then_inc(sem(st + "_centred"), 1)
                    if 1 <= g < G + 1:
                        h = g - 1
                        v.wait_ge(sem(st + "_exp"), st.at("_exp", G * i + h + 1))
                        nc.vector.tensor_reduce(rowsum[:, h % 4, :], probs[:, h % 4, :, :], AX.X, ALU.add).then_inc(
                            sem(st + "_rowsum"), 1)
                        v.wait_ge(sem(st + "_rowsum"), st.at("_rowsum", 2 * G * i + 2 * h + 1))
                        nc.vector.tensor_scalar_max(rowsum[:, h % 4, :], rowsum[:, h % 4, :], TINY).then_inc(
                            sem(st + "_rowsum"), 1)
                        v.wait_ge(sem(st + "_rowsum"), st.at("_rowsum", 2 * G * i + 2 * h + 2))
                        nc.vector.reciprocal(rowinv[:, h % 4, :], rowsum[:, h % 4, :]).then_inc(sem(st + "_rowinv"), 1)
                    if g >= 4:
                        h = g - 4
                        v.wait_ge(sem(st + "_yh"), st.at("_yh", G * i + h + 1))
                        nc.vector.tensor_tensor(yl[:, :, h * QW:(h + 1) * QW],
                                                banks[6 + h % 2][:, 0:8 * QW].rearrange("p (j w) -> p j w", w=QW),
                                                yh[:, :, h * QW:(h + 1) * QW].bitcast(F32), ALU.subtract).then_inc(
                            sem(st + "_yl"), 1)
                v.wait_ge(sem(st + "_wo"), st.at("_wo", i + 1))
                xb = x_tok[:, bass.ds(TPB * i, TPB), :]
                nc.vector.tensor_tensor(xb, xb, banks[1][:, :].rearrange("p (t d) -> p t d", d=D),
                                        ALU.add).then_inc(x_done(n), 1)

        def rwkv_sp(sp, n, st, m):
            if n:
                sp.wait_ge(x_done(n - 1), x_at(n - 1, NBLK))
            sp.dma_start(mix_raw[:, :], rwkv_pack).then_inc(sem(st + "_raw_in"), 16)
            sp.dma_start(mix_cols[:, :], rwkv_cols).then_inc(sem(st + "_raw_in"), 16)

        def rwkv_pool(pool, n, st, m):
            if n:
                pool.wait_ge(x_done(n - 1), x_at(n - 1, NBLK))
            zero = [(xs_h[:, :, 0:1].bitcast(F32), 0.0), (xs_l[:, :, 0:1].bitcast(F32), 0.0), (mm[:, :, 0:1], NEG_INF),
                    (pp[:, :, 0:1], NEG_INF), (aa[:, :, 0:1], 0.0)]
            for k, (x, value) in enumerate(zero):
                pool.memset(x, value).then_inc(sem(st + "_pad"), 1)
                pool.wait_ge(sem(st + "_pad"), st.at("_pad", k + 1))
            for b in range(NBLK):
                rstd_pool(pool, st, "_in", b)
                rstd_pool(pool, st, "_ln1", b)
            for b in range(NBLK):
                rstd_pool(pool, st, "_ln2", b)
                pool.wait_ge(sem(st + "_x1"), st.at("_x1", b + 1))
                xb, x1 = x_tok[:, TPB * b:TPB * (b + 1), :], xin[:, TPB * b:TPB * (b + 1), :]
                pool.tensor_tensor(xb, xb, x1, ALU.add).then_inc(sem(st + "_x_x1"), 1)

        def seqs(b):
            return slice(2 * b, 2 * b + 2)

        def two(ap):
            return ap.rearrange("p (s t) -> p s t", s=2)

        def rwkv_act(act, n, st, m):
            act.wait_ge(sem(st + "_raw_in"), st.at("_raw_in", 32))

            def affine_hi(bank, g, name, count):
                act.wait_ge(sem(st + name + "T"), st.at(name + "T", count + 1))
                if count:
                    act.wait_ge(sem(st + name + "_lo"), st.at(name + "_lo", count))
                act.activation(xf[:, :, :], two(bank[:, :]), ACT.Identity, scale=mix_cols[:, g:g + 1],
                               bias=mix_cols[:, g + 1:g + 2]).then_inc(sem(st + name + "_f"), 1)
                act.wait_ge(sem(st + name + "_f"), st.at(name + "_f", count + 1))
                act.activation(xs_h[:, seqs(count), 1:T + 1], xf[:, :, :], ACT.Copy).then_inc(
                    sem(st + name + "_hi"), 1)

            for b in range(NBLK):
                affine_hi(TR, C_G1, "_xa", b)
                for j, (dst, f) in enumerate(((kf, ACT.Copy), (vf, ACT.Copy), (sr, ACT.Sigmoid))):
                    act.wait_ge(sem(st + "_kvr"), st.at("_kvr", 3 * b + j + 1))
                    act.activation(dst[:, seqs(b), :], two(banks[j][:, :]), f).then_inc(sem(st + "_kvr_read"), 1)
            for b in range(NBLK):
                for r in range(2):
                    act.wait_ge(sem(st + "_clip"), st.at("_clip", 2 * b + r + 1))
                    act.activation(t1[:, :, :], t1[:, :, :], ACT.Exp, scale=-1.0)
                    act.activation(t2[:, :, :], t2[:, :, :], ACT.Exp).then_inc(sem(st + "_decay"), 1)
                    if r == 0:
                        act.wait_ge(sem(st + "_ss"), st.at("_ss", b + 1))
                        act.activation(ss[:, :, :], ss[:, :, :], ACT.Ln).then_inc(sem(st + "_ln_ss"), 1)
            for b in range(NBLK):
                act.wait_ge(sem(st + "_va"), st.at("_va", b + 1))
                if b:
                    act.wait_ge(sem(st + "_z"), st.at("_z", b))
                act.activation(q_mix[:, :, :], gap_kp[:, seqs(b), :], ACT.Sigmoid,
                               bias=mix_cols[:, C_U:C_U + 1]).then_inc(sem(st + "_q"), 1)

            def head(b):
                affine_hi(banks[7], C_G2, "_xb", b)

            def body(b):
                act.wait_ge(sem(st + "_cr"), st.at("_cr", b + 1))
                if b:
                    act.wait_ge(sem(st + "_out_c"), st.at("_out_c", b))
                act.activation(sig_c[:, :], banks[2][:, :], ACT.Sigmoid).then_inc(sem(st + "_sig_c"), 1)
                for c in range(HC):
                    k = HC * b + c
                    act.wait_ge(sem(st + "_ck"), st.at("_ck", k + 1))
                    if later(k - 1):
                        act.wait_ge(sem(st + "_kc"), st.at("_kc", k - 1))
                    act.activation(relu[:, k % 2, :], banks[k % 2][:, :], ACT.Relu).then_inc(sem(st + "_relu"), 1)
                    act.wait_ge(sem(st + "_kc"), st.at("_kc", k + 1))
                    if later(k - 1):
                        act.wait_ge(sem(st + "_cv"), st.at("_cv", k - 1))
                    act.activation(kc_h[:, k % 2, :], kc[:, k % 2, :], ACT.Copy).then_inc(sem(st + "_kc_hi"), 1)

            head(0)
            for b in range(NBLK):
                if b + 1 < NBLK:
                    head(b + 1)
                body(b)

        def rwkv_pe(pe, n, st, m):
            def shifted(dst, cols, b):
                three(pe, dst, mix_h[:, 0, cols], mix_l[:, 0, cols], xs_h[:, seqs(b), 1:T + 1],
                      xs_l[:, seqs(b), 1:T + 1], stop=False)
                return three(pe, dst, mix_h[:, 1, cols], mix_l[:, 1, cols], xs_h[:, seqs(b), 0:T],
                             xs_l[:, seqs(b), 0:T], start=False)

            def transposes(dst, src):
                for t in range(TPB):
                    ins = nc.tensor.transpose(dst[:, t * P:(t + 1) * P], src(t), ident[:, :])
                return ins

            if n:
                pe.wait_ge(x_done(n - 1), x_at(n - 1, NBLK))
            pe.wait_ge(sem(st + "_pad"), st.at("_pad", 5))
            for b in range(NBLK):
                pe.wait_ge(sem(st + "_ln1_norm"), st.at("_ln1_norm", b + 1))
                if b:
                    pe.wait_ge(sem(st + "_xa_f"), st.at("_xa_f", b))
                transposes(TR, lambda t: xn_tok[:, 0, t, :]).then_inc(sem(st + "_xaT"), 1)
                pe.wait_ge(sem(st + "_xa_lo"), st.at("_xa_lo", b + 1))
                if b == 0:
                    pe.wait_ge(sem(st + "_w_ready"), st.at("_w_ready", 1))
                for j, c in enumerate((KW, VW, RW)):
                    if later(3 * (b - 1) + j + 1):
                        pe.wait_ge(sem(st + "_kvr_read"), st.at("_kvr_read", 3 * (b - 1) + j + 1))
                    shifted(banks[j][:, :], slice(c, c + P), b).then_inc(sem(st + "_kvr"), 1)

            def head(b):
                pe.wait_ge(sem(st + "_z"), st.at("_z", b + 1))
                if b == 0:
                    pe.wait_ge(sem(st + "_xa_f"), st.at("_xa_f", NBLK))
                else:
                    pe.wait_ge(sem(st + "_x1"), st.at("_x1", b))
                if b >= 2:
                    pe.wait_ge(x_done(n), x_at(n, b - 1))
                transposes(TR, lambda t: zf[:, 2 * b + t // 2, t % 2 * P:(t % 2 + 1) * P]).then_inc(sem(st + "_zT"), 1)
                pe.wait_ge(sem(st + "_ln2_norm"), st.at("_ln2_norm", b + 1))
                if b:
                    pe.wait_ge(sem(st + "_xb_f"), st.at("_xb_f", b))
                transposes(banks[7], lambda t: xn_tok[:, 0, t, :]).then_inc(sem(st + "_xbT"), 1)

            def body(b):
                pe.wait_ge(sem(st + "_xb_lo"), st.at("_xb_lo", b + 1))
                if b == 0:
                    pe.wait_ge(sem(st + "_kvr_read"), st.at("_kvr_read", 3 * NBLK))
                else:
                    pe.wait_ge(sem(st + "_sig_c"), st.at("_sig_c", b))
                shifted(banks[2][:, :], slice(CRW, CRW + P), b).then_inc(sem(st + "_cr"), 1)

                def up(c):
                    k = HC * b + c
                    if later(k - 1):
                        pe.wait_ge(sem(st + "_relu"), st.at("_relu", k - 1))
                    shifted(banks[k % 2][:, :], slice(CKW + c * P, CKW + (c + 1) * P), b).then_inc(sem(st + "_ck"), 1)

                def down(c):
                    k = HC * b + c
                    pe.wait_ge(sem(st + "_kc_lo"), st.at("_kc_lo", k + 1))
                    if c == 0:
                        if later(b - 1):
                            pe.wait_ge(sem(st + "_out_c"), st.at("_out_c", b - 1))
                    three(pe, banks[4 + b % 2][:, :], cv_h[:, c * P:(c + 1) * P], cv_l[:, c * P:(c + 1) * P],
                          kc_h[:, k % 2, :], kc_l[:, k % 2, :], start=c == 0, stop=c == HC - 1).then_inc(
                        sem(st + "_cv"), 1)

                up(0)
                up(1)
                for c in range(HC):
                    down(c)
                    if c + 2 < HC:
                        up(c + 2)
                pe.wait_ge(sem(st + "_out_c"), st.at("_out_c", b + 1))
                pe.wait_ge(sem(st + "_x1"), st.at("_x1", min(b + 2, NBLK)))
                transposes(TR, lambda t: out_c[:, t * P:(t + 1) * P]).then_inc(sem(st + "_outT"), 1)

            head(0)
            for b in range(NBLK):
                if b + 1 < NBLK:
                    if b:
                        pe.wait_ge(x_done(n), x_at(n, b))
                    head(b + 1)
                body(b)

        def rwkv_dve(v, n, st, m):
            v.wait_ge(sem(st + "_raw_in"), st.at("_raw_in", 32))
            if n:
                v.wait_ge(x_done(n - 1), x_at(n - 1, NBLK))
            link(nc.vector.tensor_scalar(one_minus[:, :], mix_cols[:, C_RK:C_RK + 5], -1.0, 1.0, ALU.mult, ALU.add))
            places = ((KW, VW), (VW, RW), (RW, CKW), (CKW, CRW), (CRW, CVW))
            for side in range(2):
                for j, (lo, hi) in enumerate(places):
                    scale = mix_cols[:, C_RK + j:C_RK + j + 1] if side == 0 else one_minus[:, j:j + 1]
                    ins = nc.vector.tensor_scalar_mul(mix_f[:, lo:hi], mix_raw[:, lo:hi], scale)
                link(ins)
                link(nc.vector.tensor_copy(mix_h[:, side, :], mix_f[:, :]))
                link(nc.vector.tensor_tensor(mix_l[:, side, :], mix_f[:, :], mix_h[:, side, :].bitcast(F32),
                                             ALU.subtract))
            link(nc.vector.tensor_copy(cv_h[:, :], mix_raw[:, CVW:RWKV_COLS]))
            nc.vector.tensor_tensor(cv_l[:, :], mix_raw[:, CVW:RWKV_COLS], cv_h[:, :].bitcast(F32),
                                    ALU.subtract).then_inc(sem(st + "_w_ready"), 1)

            def rest(name, b):
                v.wait_ge(sem(st + name + "_hi"), st.at(name + "_hi", b + 1))
                nc.vector.tensor_tensor(xs_l[:, seqs(b), 1:T + 1], xf[:, :, :], xs_h[:, seqs(b), 1:T + 1].bitcast(F32),
                                        ALU.subtract).then_inc(sem(st + name + "_lo"), 1)

            for b in range(NBLK):
                if n == 0:
                    v.wait_ge(x_done(-1), x_at(-1, NBLK))
                link(layernorm(v, st, "_in", lambda t: x_tok[:, TPB * b + t, :], b,
                               lambda t: xin[:, TPB * b + t, :]))
                if b:
                    v.wait_ge(sem(st + "_xaT"), st.at("_xaT", b))
                layernorm(v, st, "_ln1", lambda t: xin[:, TPB * b + t, :], b).then_inc(sem(st + "_ln1_norm"), 1)
                rest("_xa", b)
            v.wait_ge(sem(st + "_pad"), st.at("_pad", 5))
            for b in range(NBLK):
                k, vv, gp = kf[:, seqs(b), :], vf[:, seqs(b), :], gap_kp[:, seqs(b), :]
                w = mix_cols[:, C_W:C_W + 1].broadcast_to([P, T])
                v.wait_ge(sem(st + "_kvr_read"), st.at("_kvr_read", 3 * b + 3))
                for s in range(2):
                    ins = nc.vector.tensor_tensor_scan(mm[:, s, 1:T + 1], kf[:, 2 * b + s, :], w, NEG_INF, ALU.max,
                                                       ALU.add)
                link(ins)

                def clips(gap):
                    nc.vector.tensor_scalar_max(t1[:, :, :], gap, 0.0)
                    nc.vector.tensor_scalar_min(t2[:, :, :], gap, 0.0).then_inc(sem(st + "_clip"), 1)

                link(nc.vector.tensor_tensor(gp, k, mm[:, :, 0:T], ALU.subtract))
                clips(gp)
                v.wait_ge(sem(st + "_decay"), st.at("_decay", 2 * b + 1))
                for s in range(2):
                    ins = nc.vector.tensor_tensor_scan(ss[:, s, :], t1[:, s, :], t2[:, s, :], 1.0, ALU.mult, ALU.add)
                ins.then_inc(sem(st + "_ss"), 1)
                v.wait_ge(sem(st + "_ln_ss"), st.at("_ln_ss", b + 1))
                link(nc.vector.tensor_tensor(pp[:, :, 1:T + 1], mm[:, :, 1:T + 1], ss[:, :, :], ALU.add))
                link(nc.vector.tensor_tensor(gp, k, pp[:, :, 0:T], ALU.subtract))
                clips(gp)
                v.wait_ge(sem(st + "_decay"), st.at("_decay", 2 * b + 2))
                link(nc.vector.tensor_tensor(t2[:, :, :], t2[:, :, :], vv, ALU.mult))
                for s in range(2):
                    ins = nc.vector.tensor_tensor_scan(aa[:, s, 1:T + 1], t1[:, s, :], t2[:, s, :], 0.0, ALU.mult,
                                                       ALU.add)
                link(ins)
                nc.vector.tensor_copy(y_mix[:, seqs(b), :], aa[:, :, 0:T])
                nc.vector.tensor_tensor(vv, vv, aa[:, :, 0:T], ALU.subtract).then_inc(sem(st + "_va"), 1)
            for b in range(NBLK):
                y, z = y_mix[:, seqs(b), :], zf[:, seqs(b), :]
                v.wait_ge(sem(st + "_q"), st.at("_q", b + 1))
                link(nc.vector.tensor_tensor(z, q_mix[:, :, :], vf[:, seqs(b), :], ALU.mult))
                link(nc.vector.tensor_tensor(z, z, y, ALU.add))
                nc.vector.tensor_tensor(z, z, sr[:, seqs(b), :], ALU.mult).then_inc(sem(st + "_z"), 1)

            def head(b):
                v.wait_ge(sem(st + "_zT"), st.at("_zT", b + 1))
                x1 = xin[:, TPB * b:TPB * (b + 1), :]
                nc.vector.tensor_tensor(x1, x1, TR[:, :].rearrange("p (t d) -> p t d", d=D), ALU.add).then_inc(
                    sem(st + "_x1"), 1)
                v.wait_ge(sem(st + "_x1"), st.at("_x1", b + 1))
                if b == 0:
                    v.wait_ge(sem(st + "_xaT"), st.at("_xaT", NBLK))
                else:
                    v.wait_ge(sem(st + "_xbT"), st.at("_xbT", b))
                layernorm(v, st, "_ln2", lambda t: xin[:, TPB * b + t, :], b).then_inc(sem(st + "_ln2_norm"), 1)
                rest("_xb", b)

            def body(b):
                for c in range(HC):
                    k = HC * b + c
                    v.wait_ge(sem(st + "_relu"), st.at("_relu", k + 1))
                    if later(k - 1):
                        v.wait_ge(sem(st + "_kc_lo"), st.at("_kc_lo", k - 1))
                    nc.vector.tensor_tensor(kc[:, k % 2, :], relu[:, k % 2, :], relu[:, k % 2, :], ALU.mult).then_inc(
                        sem(st + "_kc"), 1)
                    v.wait_ge(sem(st + "_kc_hi"), st.at("_kc_hi", k + 1))
                    nc.vector.tensor_tensor(kc_l[:, k % 2, :], kc[:, k % 2, :], kc_h[:, k % 2, :].bitcast(F32),
                                            ALU.subtract).then_inc(sem(st + "_kc_lo"), 1)
                v.wait_ge(sem(st + "_cv"), st.at("_cv", HC * (b + 1)))
                v.wait_ge(sem(st + "_sig_c"), st.at("_sig_c", b + 1))
                if b:
                    v.wait_ge(sem(st + "_outT"), st.at("_outT", b))
                nc.vector.tensor_tensor(out_c[:, :], banks[4 + b % 2][:, :], sig_c[:, :], ALU.mult).then_inc(
                    sem(st + "_out_c"), 1)
                v.wait_ge(sem(st + "_outT"), st.at("_outT", b + 1))
                v.wait_ge(sem(st + "_x_x1"), st.at("_x_x1", b + 1))
                xb = x_tok[:, TPB * b:TPB * (b + 1), :]
                nc.vector.tensor_tensor(xb, xb, TR[:, :].rearrange("p (t d) -> p t d", d=D), ALU.add).then_inc(
                    x_done(n), 1)

            head(0)
            for b in range(NBLK):
                if b + 1 < NBLK:
                    head(b + 1)
                body(b)

        GLU, MLP = Moe("glu", True), Moe("mlp", False)
        parts = {"rwkv": (None, rwkv_sp, rwkv_pool, rwkv_act, rwkv_pe, rwkv_dve),
                 "attn": (None, attn_sp, attn_pool, attn_act, attn_pe, attn_dve),
                 "glu": (GLU, moe_sp, moe_pool, moe_act, moe_pe, moe_dve),
                 "mlp": (MLP, moe_sp, moe_pool, moe_act, moe_pe, moe_dve)}

        @block.sync
        def _(sp):
            for b in range(NBLK):
                sp.dma_start(x_tok[:, TPB * b:TPB * (b + 1), :],
                             x_in.rearrange("b (t p) d -> p (b t) d", p=P)[:, TPB * b:TPB * (b + 1), :]).then_inc(
                    sem("x_loaded"), 16)
            sp.dma_start(gate_raw["glu"][:, :], glu_gate).then_inc(sem("small_in"), 16)
            sp.dma_start(gate_raw["mlp"][:, :], mlp_gate).then_inc(sem("small_in"), 16)
            sp.dma_start(shared_raw[:, :], mlp_shared).then_inc(sem("small_in"), 16)
            sp.dma_start(gate_bias[:, :], glu_gate_b.broadcast_to([P, E])).then_inc(sem("small_in"), 16)
            sp.dma_start(half_gamma[:, :], mlp_rows[0:1, :].broadcast_to([P, D])).then_inc(sem("small_in"), 16)
            sp.dma_start(half_beta[:, :], mlp_rows[1:2, :].broadcast_to([P, D])).then_inc(sem("small_in"), 16)
            for n, (st, kind) in enumerate(order):
                parts[kind][1](sp, n, st, parts[kind][0])
            for b in range(NBLK):
                sp.wait_ge(x_done(len(order) - 1), x_at(len(order) - 1, b + 1))
                sp.dma_start(out.rearrange("b (t p) d -> p (b t) d", p=P)[:, TPB * b:TPB * (b + 1), :],
                             x_tok[:, TPB * b:TPB * (b + 1), :]).then_inc(sem("stored"), 16)
            sp.wait_ge(sem("stored"), 16 * NBLK)

        @block.gpsimd
        def _(pool):
            pool.memset(ident[:, :], 0.0).then_inc(sem("ident_zero"), 1)
            pool.memset(one[:, :], 1.0)
            pool.memset(neghalf[:, :], -0.5).then_inc(sem("neghalf_set"), 1)
            pool.wait_ge(sem("ident_zero"), 1)
            pool.affine_select(out=ident[:, :], in_=ident[:, :], compare_op=ALU.not_equal, fill=1.0, base=0,
                               pattern=[[-1, P]], channel_multiplier=1).then_inc(sem("ident_set"), 1)
            pool.wait_ge(sem("neghalf_set"), 1)
            steps = [0]

            def then(ins):
                steps[0] += 1
                ins.then_inc(sem("mask_step"), 1)
                pool.wait_ge(sem("mask_step"), steps[0])

            then(pool.memset(mask[:, :, :], 0.0))
            for r in range(4):
                rows = mask[r * QW:(r + 1) * QW, :, 0:2 * QW]
                then(pool.affine_select(out=rows, in_=rows, compare_op=ALU.is_ge, fill=MASKED, base=QW,
                                        pattern=[[0, 3], [-1, 2 * QW]], channel_multiplier=1))
                then(pool.affine_select(out=rows, in_=rows, compare_op=ALU.is_ge, fill=MASKED, base=-1,
                                        pattern=[[0, 3], [1, 2 * QW]], channel_multiplier=-1))
                rows = mask[r * QW:(r + 1) * QW, 0, 2 * QW:KEYS]
                then(pool.affine_select(out=rows, in_=rows, compare_op=ALU.is_ge, fill=MASKED, base=0,
                                        pattern=[[-1, SINK]], channel_multiplier=1))
            then(pool.memset(mask[:, 0, 0:QW + SINK], MASKED))
            then(pool.memset(mask[:, 1, 0:SINK], MASKED))
            for n, (st, kind) in enumerate(order):
                parts[kind][2](pool, n, st, parts[kind][0])

        @block.scalar
        def _(act):
            for n, (st, kind) in enumerate(order):
                parts[kind][3](act, n, st, parts[kind][0])

        @block.tensor
        def _(pe):
            pe.wait_ge(sem("ident_set"), 1)
            for n, (st, kind) in enumerate(order):
                parts[kind][4](pe, n, st, parts[kind][0])

        @block.vector
        def _(v):
            for e in range(E):
                ins = nc.vector.memset(iota8[:, e:e + 1], float(e))
            link(ins)
            v.wait_ge(sem("small_in"), 16 * 6)
            v.wait_ge(sem("mask_step"), 15)
            nc.vector.tensor_scalar_mul(half_gamma[:, :], half_gamma[:, :], 0.5)
            nc.vector.tensor_scalar_mul(half_beta[:, :], half_beta[:, :], 0.5)
            for g in ("glu", "mlp"):
                link(nc.vector.tensor_copy(gate_h[g][:, :], gate_raw[g][:, :]))
                nc.vector.tensor_tensor(gate_l[g][:, :], gate_raw[g][:, :], gate_h[g][:, :].bitcast(F32), ALU.subtract)
            link(nc.vector.tensor_copy(shared_h[:, :], shared_raw[:, 0:D]))
            nc.vector.tensor_tensor(shared_l[:, :], shared_raw[:, 0:D], shared_h[:, :].bitcast(F32),
                                    ALU.subtract).then_inc(sem("const_ready"), 1)
            for n, (st, kind) in enumerate(order):
                parts[kind][5](v, n, st, parts[kind][0])


def _layout(i):
    import numpy as np

    def a(name):
        return np.ascontiguousarray(np.asarray(i[name]))

    def col(v):
        return v.reshape(-1, 128).T

    def pack(ups, down, biases):
        per = []
        for e in range(E):
            down_e = down[e].reshape(HC, 128, 128).transpose(1, 0, 2).reshape(128, 512)
            per.append(np.concatenate([u[e] for u in ups] + [down_e] + [col(b[e]) for b in biases], axis=1))
        return np.ascontiguousarray(np.concatenate(per, axis=1))

    glu = pack([a("L0_ffn_W0"), a("L0_ffn_W1")], a("L0_ffn_W2"), [a("L0_ffn_b0"), a("L0_ffn_b1"), a("L0_ffn_b2")])
    mlp = pack([a("L1_ffn_W1")], a("L1_ffn_W2"), [a("L1_ffn_b1"), a("L1_ffn_b2")])
    shared = np.concatenate([a("L1_ffn_shared_W"), col(a("L1_ffn_shared_b"))], axis=1)
    wq = a("L0_attn_Wq").reshape(D, 2, 2, 4, HD).transpose(0, 1, 3, 2, 4).reshape(D, 1024)
    wo = a("L0_attn_Wo").reshape(2, 2, 4, HD, D).transpose(1, 3, 0, 2, 4).reshape(D, 1024)
    attn = np.concatenate([wq, a("L0_attn_Wk"), a("L0_attn_Wv"), wo], axis=1)
    cv = a("L1_attn_Wcv").T.reshape(HC, 128, 128).transpose(1, 0, 2).reshape(128, 512)
    rwkv = np.concatenate([a("L1_attn_Wk").T, a("L1_attn_Wv").T, a("L1_attn_Wr").T, a("L1_attn_Wck").T,
                           a("L1_attn_Wcr").T, cv], axis=1)
    cols = np.stack([a("L1_attn_" + n) for n in ("w", "u", "rk", "rv", "rr", "crk", "crr", "ln1_g", "ln1_b", "ln2_g",
                                                 "ln2_b")], axis=1)
    rows = np.stack([a("L1_ffn_gamma"), a("L1_ffn_beta")])
    return {
        "x_in": a("L0_attn_X"), "glu_pack": glu, "glu_gate": a("L0_ffn_Wg"), "glu_gate_b": a("L0_ffn_bg")[None, :],
        "mlp_pack": mlp, "mlp_gate": a("L1_ffn_gate_W"), "mlp_shared": shared, "mlp_rows": rows,
        "attn_pack": attn, "rwkv_pack": rwkv, "rwkv_cols": cols,
    }


def kernel(**inputs):
    import concourse.bacc as bacc
    from concourse.bass_utils import run_bass_kernel_spmd

    nc = bacc.Bacc("TRN2", target_bir_lowering=False, num_devices=1)
    arrays = _layout(inputs)
    args = [nc.dram_tensor(n, x.shape, mybir.dt.from_np(x.dtype), kind="ExternalInput").ap()
            for n, x in arrays.items()]
    args.append(nc.dram_tensor("out", (B, T, D), F32, kind="ExternalOutput").ap())
    build_program(nc, *args)
    return run_bass_kernel_spmd(nc, [arrays], core_ids=[0]).results[0]["out"]
```
